# Optimizing a Trainium2 kernel written in Bass

```python
import numpy as np
import jax
import jax.numpy as jnp

def _softmax(x, axis=-1):
    return jax.nn.softmax(x, axis=axis)

def _gelu(x):
    return jax.nn.gelu(x, approximate=True)

def _silu(x):
    return jax.nn.silu(x)

def _sigmoid(x):
    return jax.nn.sigmoid(x)

def _layernorm(x, axis=-1, eps=1e-05):
    m = jnp.mean(x, axis=axis, keepdims=True)
    v = jnp.var(x, axis=axis, keepdims=True)
    return (x - m) / jnp.sqrt(v + eps)

def _scatter_add(tgt, idx, src, axis=0):
    return tgt.at[idx].add(src)

def _segment_sum(src, seg, n):
    return jax.ops.segment_sum(src, seg, n)
kernel_name = 'mk_macaron_d1_jaxref_r4_a65c74'

def setup_inputs(seed: int=0):
    np.random.seed(seed)
    _w = jnp.asarray

    def _L0_attn_setup():
        import jax, jax.numpy as jnp
        import numpy as np
        B, N, D = (2, 1024, 256)
        H, Dh = (8, 64)
        INNER = H * Dh
        W = 64
        NQ = NKV = 256

        def _forward(x, gamma_h, wq_h, wkv_h, wo_h, ln_g, ln_b, wqkv_l, wo_l, rt_q, rt_kv):
            b, n, d = x.shape
            scale = Dh ** (-0.5)
            neg = -jnp.finfo(x.dtype).max
            mu = jnp.mean(x, -1, keepdims=True)
            var = jnp.var(x, -1, keepdims=True)
            xl = (x - mu) / jnp.sqrt(var + 1e-05) * ln_g + ln_b
            q, k, v = jnp.split(xl @ wqkv_l, 3, -1)

            def heads(t):
                return t.reshape(b, n, H, Dh).transpose(0, 2, 1, 3)
            q, k, v = (heads(q), heads(k), heads(v))
            nw = n // W
            qw = q.reshape(b, H, nw, W, Dh)

            def look_around(t):
                tw = t.reshape(b, H, nw, W, Dh)
                tp = jnp.pad(tw, ((0, 0), (0, 0), (1, 1), (0, 0), (0, 0)))
                return jnp.concatenate([tp[:, :, s:s + nw] for s in range(3)], axis=3)
            kk, vv = (look_around(k), look_around(v))
            wi = jnp.arange(nw)[:, None]
            sh = jnp.arange(3)[None, :]
            valid = (wi + sh - 1 >= 0) & (wi + sh - 1 < nw)
            valid = jnp.repeat(valid, W, axis=1)
            sim = jnp.einsum('bhnid,bhnjd->bhnij', qw * scale, kk)
            sim = jnp.where(valid[None, None, :, None, :], sim, neg)
            attn = jax.nn.softmax(sim, axis=-1)
            lo = jnp.einsum('bhnij,bhnjd->bhnid', attn, vv)
            light_out = lo.reshape(b, H, n, Dh).transpose(0, 2, 1, 3).reshape(b, n, INNER) @ wo_l

            def route(rt, num):
                scores = jnp.einsum('bnd,d->bn', x, rt)
                idx = jnp.argsort(scores, axis=-1)
                s = jnp.take_along_axis(scores, idx, -1)
                s = s - jax.lax.stop_gradient(jnp.max(s, -1, keepdims=True))
                e = jnp.exp(s)
                cs = e / jnp.clip(jnp.cumsum(e, -1), 1e-06, None)
                sel_s, sel_i = (cs[:, -num:], idx[:, -num:])
                sel_s = sel_s + jax.lax.stop_gradient(1.0 - sel_s)
                return (sel_s, sel_i)
            sq, iq = route(rt_q, NQ)
            skv, ikv = route(rt_kv, NKV)
            rq = jnp.take_along_axis(x, iq[:, :, None], 1)
            rkv = jnp.take_along_axis(x, ikv[:, :, None], 1)

            def rms(t):
                t = t / jnp.clip(jnp.linalg.norm(t, axis=-1, keepdims=True), 1e-12, None)
                return t * d ** 0.5 * gamma_h
            hq = (rms(rq) @ wq_h).reshape(b, NQ, H, Dh).transpose(0, 2, 1, 3)
            hk, hv = jnp.split(rms(rkv) @ wkv_h, 2, -1)
            hk = hk.reshape(b, NKV, H, Dh).transpose(0, 2, 1, 3)
            hv = hv.reshape(b, NKV, H, Dh).transpose(0, 2, 1, 3)
            hv = hv * skv[:, None, :, None]
            hsim = jnp.einsum('bhid,bhjd->bhij', hq * scale, hk)
            hattn = jax.nn.softmax(hsim, axis=-1)
            ho = jnp.einsum('bhij,bhjd->bhid', hattn, hv)
            ho = ho.transpose(0, 2, 1, 3).reshape(b, NQ, INNER) @ wo_h
            ho = ho * sq[:, :, None]
            heavy_out = jnp.zeros_like(x).at[jnp.arange(b)[:, None], iq].set(ho)
            return light_out + heavy_out
        key = jax.random.key(seed)
        ks = jax.random.split(key, 8)
        std = 0.02
        return {'x': jax.random.normal(ks[0], (B, N, D), jnp.float32), 'gamma_h': jnp.ones((D,), jnp.float32), 'wq_h': jax.random.normal(ks[1], (D, INNER), jnp.float32) * std, 'wkv_h': jax.random.normal(ks[2], (D, 2 * INNER), jnp.float32) * std, 'wo_h': jax.random.normal(ks[3], (INNER, D), jnp.float32) * std, 'ln_g': jnp.ones((D,), jnp.float32), 'ln_b': jnp.zeros((D,), jnp.float32), 'wqkv_l': jax.random.normal(ks[4], (D, 3 * INNER), jnp.float32) * std, 'wo_l': jax.random.normal(ks[5], (INNER, D), jnp.float32) * std, 'rt_q': jax.random.normal(ks[6], (D,), jnp.float32), 'rt_kv': jax.random.normal(ks[7], (D,), jnp.float32)}
    _L0_attn_in = _L0_attn_setup()

    def _L0_ffn_setup():
        import jax, jax.numpy as jnp
        import numpy as np
        D_MODEL = 256
        D_FF = 1024
        N_EXPERTS = 8
        TOP_K = 2
        D_FF_PER = D_FF // N_EXPERTS
        B, T = (4, 512)
        key = jax.random.key(seed)
        ks = jax.random.split(key, 7)
        b1_bound = 1.0 / np.sqrt(D_MODEL)
        b2_bound = 1.0 / np.sqrt(D_FF_PER)
        return {'x': jax.random.normal(ks[0], (B, T, D_MODEL), dtype=jnp.float32), 'router_w': jax.random.uniform(ks[1], (D_MODEL, N_EXPERTS), minval=-b1_bound, maxval=b1_bound, dtype=jnp.float32), 'router_b': jax.random.uniform(ks[2], (N_EXPERTS,), minval=-b1_bound, maxval=b1_bound, dtype=jnp.float32), 'W1': jax.random.uniform(ks[3], (N_EXPERTS, D_MODEL, D_FF_PER), minval=-b1_bound, maxval=b1_bound, dtype=jnp.float32), 'b1': jax.random.uniform(ks[4], (N_EXPERTS, D_FF_PER), minval=-b1_bound, maxval=b1_bound, dtype=jnp.float32), 'W2': jax.random.uniform(ks[5], (N_EXPERTS, D_FF_PER, D_MODEL), minval=-b2_bound, maxval=b2_bound, dtype=jnp.float32), 'b2': jax.random.uniform(ks[6], (N_EXPERTS, D_MODEL), minval=-b2_bound, maxval=b2_bound, dtype=jnp.float32)}
    _L0_ffn_in = _L0_ffn_setup()
    _d = {'L0_attn_x': _L0_attn_in['x'], 'L0_attn_gamma_h': _L0_attn_in['gamma_h'], 'L0_attn_wq_h': _L0_attn_in['wq_h'], 'L0_attn_wkv_h': _L0_attn_in['wkv_h'], 'L0_attn_wo_h': _L0_attn_in['wo_h'], 'L0_attn_ln_g': _L0_attn_in['ln_g'], 'L0_attn_ln_b': _L0_attn_in['ln_b'], 'L0_attn_wqkv_l': _L0_attn_in['wqkv_l'], 'L0_attn_wo_l': _L0_attn_in['wo_l'], 'L0_attn_rt_q': _L0_attn_in['rt_q'], 'L0_attn_rt_kv': _L0_attn_in['rt_kv'], 'L0_ffn_router_w': _L0_ffn_in['router_w'], 'L0_ffn_router_b': _L0_ffn_in['router_b'], 'L0_ffn_W1': _L0_ffn_in['W1'], 'L0_ffn_b1': _L0_ffn_in['b1'], 'L0_ffn_W2': _L0_ffn_in['W2'], 'L0_ffn_b2': _L0_ffn_in['b2']}
    _x0 = _d['L0_attn_x']
    _d['L0_attn_x'] = jax.random.normal(jax.random.fold_in(jax.random.key(seed), 1), (8, 1024, 256), dtype=_x0.dtype)
    del _x0
    return _d

def reference(L0_attn_x, L0_attn_gamma_h, L0_attn_wq_h, L0_attn_wkv_h, L0_attn_wo_h, L0_attn_ln_g, L0_attn_ln_b, L0_attn_wqkv_l, L0_attn_wo_l, L0_attn_rt_q, L0_attn_rt_kv, L0_ffn_router_w, L0_ffn_router_b, L0_ffn_W1, L0_ffn_b1, L0_ffn_W2, L0_ffn_b2):

    def _L0_attn_ref(x, gamma_h, wq_h, wkv_h, wo_h, ln_g, ln_b, wqkv_l, wo_l, rt_q, rt_kv):
        import jax, jax.numpy as jnp
        import numpy as np
        B, N, D = (2, 1024, 256)
        H, Dh = (8, 64)
        INNER = H * Dh
        W = 64
        NQ = NKV = 256

        def _forward(x, gamma_h, wq_h, wkv_h, wo_h, ln_g, ln_b, wqkv_l, wo_l, rt_q, rt_kv):
            b, n, d = x.shape
            scale = Dh ** (-0.5)
            neg = -jnp.finfo(x.dtype).max
            mu = jnp.mean(x, -1, keepdims=True)
            var = jnp.var(x, -1, keepdims=True)
            xl = (x - mu) / jnp.sqrt(var + 1e-05) * ln_g + ln_b
            q, k, v = jnp.split(xl @ wqkv_l, 3, -1)

            def heads(t):
                return t.reshape(b, n, H, Dh).transpose(0, 2, 1, 3)
            q, k, v = (heads(q), heads(k), heads(v))
            nw = n // W
            qw = q.reshape(b, H, nw, W, Dh)

            def look_around(t):
                tw = t.reshape(b, H, nw, W, Dh)
                tp = jnp.pad(tw, ((0, 0), (0, 0), (1, 1), (0, 0), (0, 0)))
                return jnp.concatenate([tp[:, :, s:s + nw] for s in range(3)], axis=3)
            kk, vv = (look_around(k), look_around(v))
            wi = jnp.arange(nw)[:, None]
            sh = jnp.arange(3)[None, :]
            valid = (wi + sh - 1 >= 0) & (wi + sh - 1 < nw)
            valid = jnp.repeat(valid, W, axis=1)
            sim = jnp.einsum('bhnid,bhnjd->bhnij', qw * scale, kk)
            sim = jnp.where(valid[None, None, :, None, :], sim, neg)
            attn = jax.nn.softmax(sim, axis=-1)
            lo = jnp.einsum('bhnij,bhnjd->bhnid', attn, vv)
            light_out = lo.reshape(b, H, n, Dh).transpose(0, 2, 1, 3).reshape(b, n, INNER) @ wo_l

            def route(rt, num):
                scores = jnp.einsum('bnd,d->bn', x, rt)
                idx = jnp.argsort(scores, axis=-1)
                s = jnp.take_along_axis(scores, idx, -1)
                s = s - jax.lax.stop_gradient(jnp.max(s, -1, keepdims=True))
                e = jnp.exp(s)
                cs = e / jnp.clip(jnp.cumsum(e, -1), 1e-06, None)
                sel_s, sel_i = (cs[:, -num:], idx[:, -num:])
                sel_s = sel_s + jax.lax.stop_gradient(1.0 - sel_s)
                return (sel_s, sel_i)
            sq, iq = route(rt_q, NQ)
            skv, ikv = route(rt_kv, NKV)
            rq = jnp.take_along_axis(x, iq[:, :, None], 1)
            rkv = jnp.take_along_axis(x, ikv[:, :, None], 1)

            def rms(t):
                t = t / jnp.clip(jnp.linalg.norm(t, axis=-1, keepdims=True), 1e-12, None)
                return t * d ** 0.5 * gamma_h
            hq = (rms(rq) @ wq_h).reshape(b, NQ, H, Dh).transpose(0, 2, 1, 3)
            hk, hv = jnp.split(rms(rkv) @ wkv_h, 2, -1)
            hk = hk.reshape(b, NKV, H, Dh).transpose(0, 2, 1, 3)
            hv = hv.reshape(b, NKV, H, Dh).transpose(0, 2, 1, 3)
            hv = hv * skv[:, None, :, None]
            hsim = jnp.einsum('bhid,bhjd->bhij', hq * scale, hk)
            hattn = jax.nn.softmax(hsim, axis=-1)
            ho = jnp.einsum('bhij,bhjd->bhid', hattn, hv)
            ho = ho.transpose(0, 2, 1, 3).reshape(b, NQ, INNER) @ wo_h
            ho = ho * sq[:, :, None]
            heavy_out = jnp.zeros_like(x).at[jnp.arange(b)[:, None], iq].set(ho)
            return light_out + heavy_out
        return _forward(x, gamma_h, wq_h, wkv_h, wo_h, ln_g, ln_b, wqkv_l, wo_l, rt_q, rt_kv)

    def _L0_ffn_ref(x, router_w, router_b, W1, b1, W2, b2):
        import jax, jax.numpy as jnp
        import numpy as np
        D_MODEL = 256
        D_FF = 1024
        N_EXPERTS = 8
        TOP_K = 2
        D_FF_PER = D_FF // N_EXPERTS
        B, T = (4, 512)
        router_logits = x @ router_w + router_b
        routing_weights = jax.nn.softmax(router_logits, axis=-1)
        top_k_weights, top_k_indices = jax.lax.top_k(routing_weights, TOP_K)
        top_k_weights = top_k_weights / jnp.sum(top_k_weights, axis=-1, keepdims=True)
        routing_mask = jnp.zeros_like(routing_weights)
        routing_mask = jnp.take_along_axis(routing_mask, top_k_indices, axis=-1)
        b_idx = jnp.arange(x.shape[0])[:, None, None]
        t_idx = jnp.arange(x.shape[1])[None, :, None]
        routing_mask = jnp.zeros_like(routing_weights).at[b_idx, t_idx, top_k_indices].set(top_k_weights)
        h1 = jnp.einsum('btd,nde->btne', x, W1) + b1
        h1 = jax.nn.gelu(h1, approximate=False)
        out_per_expert = jnp.einsum('btne,nef->btnf', h1, W2) + b2
        output = jnp.sum(out_per_expert * routing_mask[..., None], axis=-2)
        return output
    x = L0_attn_x
    x = x + 0.5 * _L0_ffn_ref(_layernorm(x, axis=-1), L0_ffn_router_w, L0_ffn_router_b, L0_ffn_W1, L0_ffn_b1, L0_ffn_W2, L0_ffn_b2)
    x = x + _L0_attn_ref(_layernorm(x, axis=-1), L0_attn_gamma_h, L0_attn_wq_h, L0_attn_wkv_h, L0_attn_wo_h, L0_attn_ln_g, L0_attn_ln_b, L0_attn_wqkv_l, L0_attn_wo_l, L0_attn_rt_q, L0_attn_rt_kv)
    x = x + 0.5 * _L0_ffn_ref(_layernorm(x, axis=-1), L0_ffn_router_w, L0_ffn_router_b, L0_ffn_W1, L0_ffn_b1, L0_ffn_W2, L0_ffn_b2)
    return x

_drawn_inputs = setup_inputs


def setup_inputs(seed=0):
    import zlib

    import numpy as np

    out = dict(_drawn_inputs(seed))
    spreads = {'L0_attn_gamma_h': (1.0, 0.6), 'L0_attn_ln_g': (1.0, 0.6), 'L0_attn_ln_b': (0.0, 0.492)}
    factors = {'L0_attn_wq_h': 8.0,
     'L0_attn_wkv_h': 6.786,
     'L0_attn_wo_h': 6.856,
     'L0_attn_wqkv_l': 2.879,
     'L0_attn_wo_l': 2.844,
     'L0_attn_rt_q': 8.0,
     'L0_attn_rt_kv': 7.491,
     'L0_ffn_b1': 5.954}
    for name, (base, spread) in spreads.items():
        noise = np.random.default_rng([zlib.crc32(name.encode()), seed]).standard_normal(out[name].shape)
        drawn = base * np.exp(spread * noise) if base else spread * noise
        out[name] = jnp.asarray(drawn.astype(out[name].dtype))
    for name, factor in factors.items():
        out[name] = (out[name] * factor).astype(out[name].dtype)
    return out
```

```python
from contextlib import ExitStack

import numpy as np

import concourse.bass as bass
from concourse import mybir

F32 = mybir.dt.float32
F32R = mybir.dt.float32r
BF16 = mybir.dt.bfloat16
I32 = mybir.dt.int32
ALU = mybir.AluOpType
ACT = mybir.ActivationFunctionType
AX_X = mybir.AxisListType.X

P = 128
WIN = 64
KEYS = 4 * WIN
HALO = WIN
NSEL = 256
HEADS, DH = 8, 64
TOPK = 2
LN_EPS = 1e-5
NORM_MIN = 1e-12
MASKED = -1e30


class Signal:

    def __init__(self, sem):
        self.sem, self.n = sem, 0

    def on(self, ins, by=1):
        ins.then_inc(self.sem, by)
        self.n += by
        return self.sem, self.n


def build(nc, x_in, gamma_h, wq_h, wkv_h, wo_h, ln_g, ln_b, wqkv, wo_l, rt_q, rt_kv,
          router_w, router_b, w1, b1, w2, b2, out):
    pe, act, dve, pool, sp = nc.tensor, nc.scalar, nc.vector, nc.gpsimd, nc.sync
    ROWS, N, D = x_in.shape
    E, _, FF = w1.shape
    T = N // P
    C = D // P
    INNER = HEADS * DH
    HC = INNER // P
    G = 2
    TG = T // G
    NG = TG * P
    ST = NSEL // P
    PADDED = N + 2 * HALO
    assert FF == P and KEYS == NSEL and HC == 4 and TG == 4

    ctx = ExitStack()
    with ctx:
        sems = {}

        def sig(name):
            if name not in sems:
                sems[name] = Signal(ctx.enter_context(nc.semaphore(name)))
            return sems[name]

        def need(eng, *events):
            for e in events:
                if e is None:
                    continue
                key = (str(eng.engine), str(e[0]))
                if waited.get(key, 0) < e[1]:
                    waited[key] = e[1]
                    eng.wait_ge(*e)

        waited = {}

        top = [-(-nc.sbuf_base // 64) * 64]

        def place(nbytes):
            at = top[0]
            top[0] += -(-nbytes // 64) * 64
            assert top[0] <= nc.sbuf_usable_end, top[0]
            return at

        def at(name, shape, dt, offset):
            return nc.alloc_sbuf_tensor_at(name, shape, dt, offset=offset)

        def sb(name, shape, dt=F32):
            size = int(np.prod(shape[1:])) * (2 if dt == BF16 else 4)
            return at(name, shape, dt, place(size))

        def pair(name, shape):
            return sb(name + "_hi", shape, F32R), sb(name + "_lo", shape, F32R)

        w1_s = pair("w1", [P, C, E, FF])
        w2_s = pair("w2", [P, E, D])
        wqkv_s = pair("wqkv", [P, C, 3 * INNER])
        rw_s = pair("rw", [P, C, E])
        wqh_s = sb("wqh", [P, C, INNER])
        wkvh_s = sb("wkvh", [P, C, 2 * INNER])
        wol_s = sb("wol", [P, HC, D])
        woh_s = sb("woh", [P, HC, D])
        b2_s = sb("b2s", [E, D])
        b1_s = sb("b1s", [P, E])
        rb_s = sb("rbs", [P, E])
        gam_s = sb("gams", [P, C])
        lng_s = sb("lngs", [P, C])
        lnb_s = sb("lnbs", [P, C])
        rt_s = sb("rts", [P, 2, D])
        ident = sb("ident", [P, P])
        iota_row = sb("iota_row", [P, NSEL])
        iota_col = sb("iota_col", [P, ST])
        later = sb("later", [P, P], BF16)
        not_later = sb("not_later", [P, P], BF16)
        lower_e = sb("lower_e", [P, E, E], BF16)
        minus_half = sb("minus_half", [P, TG])
        euler = sb("euler", [P, TG * E])
        shared = place(TG * P * 4)
        gT = at("gT", [E, TG, P], F32, shared)
        masks = at("masks", [98, P + 3 * KEYS], BF16, shared)
        mask_qs = [masks[r:r + 2, 0:P] for r in (32, 96)]
        mask_ks = [masks[r:r + 2, P:P + 3 * KEYS].rearrange("w (v k) -> w v k", v=3) for r in (32, 96)]

        x_off = place(N * D // P * 4)
        xin = at("xin", [P, T, D], F32, x_off)
        onehot = at("onehot", [P, T, NSEL], F32R, x_off)
        x1 = sb("x1", [P, T, D])
        yr_off = place(2 * T * D * 4)
        yr = (at("yr_hi", [P, T, D], F32R, yr_off), at("yr_lo", [P, T, D], F32R, yr_off + T * D * 4))
        rank_hot = at("rank_hot", [P, ST, N], F32R, yr_off)
        ho = (at("ho_hi", [P, ST, D], F32R, yr_off + ST * N * 4),
              at("ho_lo", [P, ST, D], F32R, yr_off + ST * N * 4 + ST * D * 4))
        xt_off = place(2 * C * PADDED * 4)
        xt = (at("xt_hi", [P, C, PADDED], F32R, xt_off),
              at("xt_lo", [P, C, PADDED], F32R, xt_off + C * PADDED * 4))
        q_off = top[0]
        qT = sb("qT", [P, HC, N])
        kT = sb("kT", [P, HC, PADDED])
        V = sb("V", [P, T + 1, INNER])
        half = HALO * 4
        hin = [at(f"hin{r}", [P, C, NSEL], F32, xt_off + half + r * C * NSEL * 4) for r in range(2)]
        hq = at("hq", [P, HC, NSEL], F32, xt_off + half + PADDED * 4)
        hk = at("hk", [P, HC, NSEL], F32, xt_off + half + 2 * PADDED * 4)
        hv = at("hv", [P, ST, INNER], F32, xt_off + half + 3 * PADDED * 4)
        NP = 3
        ring = place((NP * 2 * KEYS + 2 * 4 * P + 2 * INNER) * 4)
        hf = [at(f"hf{i}", [P, NG], F32, ring + i * NG * 4) for i in range(2)]
        hh = [at(f"hh{i}", [P, NG], F32R, ring + (2 + i) * NG * 4) for i in range(2)]
        hl = [at(f"hl{i}", [P, NG], F32R, ring + (4 + i) * NG * 4) for i in range(2)]
        srow = at("srow", [P, 2, N], F32, ring)
        junk = at("junk", [P, 2, N], mybir.dt.uint8, ring + 2 * N * 4)
        rank_row = at("rank_row", [P, N], F32, ring + (NP * 2 * KEYS + 2 * 4 * P) * 4 - 1024 * 0)
        prob = [at(f"prob{i}", [P, 2, KEYS], F32, ring + i * 2 * KEYS * 4) for i in range(NP)]
        probT = [at(f"probT{i}", [P, 4, P], F32, ring + (NP * 2 * KEYS + i * 4 * P) * 4) for i in range(2)]
        o_s = at("o_s", [P, INNER], F32, ring + (NP * 2 * KEYS + 8 * P) * 4)
        oT_s = at("oT_s", [P, HC, P], F32, ring + (NP * 2 * KEYS + 8 * P + INNER) * 4)
        y_t = sb("y_t", [P, TG, D])
        xf_t = at("xf_t", [P, C, 2 * P], F32, ring + 6 * NG * 4)
        sjunk = sb("sjunk", [P, 2, D], BF16)
        st = sb("st", [P, TG, 6])
        mv = sb("mv", [P, TG, 2])
        vt = sb("vt", [P, TG])
        rs = sb("rs", [P, TG])
        rn = sb("rn", [P, TG])
        scol = sb("scol", [P, 2, T])
        rank4 = sb("rank4", [P, 2, T, 4])
        rank = sb("rank", [P, 2, T])
        lg = sb("lg", [P, TG, E])
        cmp_g = sb("cmp_g", [P, TG, E, E], BF16)
        cmp_e = sb("cmp_e", [P, TG, E, E], BF16)
        lmax = sb("lmax", [P, TG])
        lrank = sb("lrank", [P, TG, E])
        ex = sb("ex", [P, TG, E])
        exs = sb("exs", [P, TG])
        gate = sb("gate", [P, G, TG, E])
        nmax = sb("nmax", [P, 4, 2])
        den = sb("den", [P, 2, HEADS])
        rden = sb("rden", [P, HEADS])

        bank = [ctx.enter_context(nc.psum_tensor(f"bank{i}", [P, 512], F32)) for i in range(8)]
        free = [None] * 8
        TP, MISC = 6, 7

        def bview(i, pattern, **kw):
            return bank[i][:, :].rearrange(pattern, **kw)

        def mm3(o, w, x, start=True, stop=True):
            pe.matmul(o, w[0], x[0], start=start, stop=False)
            pe.matmul(o, w[1], x[0], start=False, stop=False)
            return pe.matmul(o, w[0], x[1], start=False, stop=stop)

        def bcast_rows(v, n):
            return v.rearrange("(a n) -> a n", a=1).broadcast_to([P, n])

        wst = at("wst", [P, 2 * P * C * E + C * 3 * INNER + C * E], F32, q_off)
        loads = [
            (lambda o: o.rearrange("p (c e f) -> p c e f", c=C, e=E), w1.rearrange("e (c p) f -> p c e f", p=P), w1_s, C * E * FF),
            (lambda o: o.rearrange("p (e n) -> p e n", e=E), w2.rearrange("e p n -> p e n"), w2_s, E * D),
            (lambda o: o.rearrange("p (c n) -> p c n", c=C), wqkv.rearrange("(c p) n -> p c n", p=P), wqkv_s, C * 3 * INNER),
            (lambda o: o.rearrange("p (c n) -> p c n", c=C), router_w.rearrange("(c p) n -> p c n", p=P), rw_s, C * E),
        ]
        s_x = ctx.enter_context(nc.semaphore("x_loaded"))
        s_out = ctx.enter_context(nc.semaphore("row_stored"))
        x_v = x_in.rearrange("b (t p) d -> b p t d", p=P)
        out_v = out.rearrange("b (t p) d -> b p t d", p=P)

        x_ready = {}
        for g in range(G):
            x_ready[g] = sig(f"x_load{g}").on(sp.dma_start(xin[:, g * TG:(g + 1) * TG, :], x_v[0, :, g * TG:(g + 1) * TG, :]), 16)
        o = 0
        views = []
        for shape, src, dst, n in loads:
            v = shape(wst[:, o:o + n])
            for c in range(src.shape[1]):
                ev = sig(f"w_load{len(views)}").on(sp.dma_start(v[:, c], src[:, c]), 16)
            views.append((wst[:, o:o + n], dst, ev))
            o += n
        for dst, src in ((b1_s[:, :], b1.rearrange("e f -> f e")), (rb_s[:, :], bcast_rows(router_b, E)),
                         (b2_s[:, :], b2), (gam_s[:, :], gamma_h.rearrange("(c p) -> p c", p=P)),
                         (lng_s[:, :], ln_g.rearrange("(c p) -> p c", p=P)), (lnb_s[:, :], ln_b.rearrange("(c p) -> p c", p=P)),
                         (rt_s[:, 0, :], bcast_rows(rt_q, D)), (rt_s[:, 1, :], bcast_rows(rt_kv, D)),
                         (wqh_s[:, :, :], wq_h.rearrange("(c p) n -> p c n", p=P)),
                         (wkvh_s[:, :, :], wkv_h.rearrange("(c p) n -> p c n", p=P)),
                         (wol_s[:, :, :], wo_l.rearrange("(c p) n -> p c n", p=P)),
                         (woh_s[:, :, :], wo_h.rearrange("(c p) n -> p c n", p=P))):
            small = sig("c_load").on(act.dma_start(dst, src, allow_slow_non_contiguous=True), 16)

        def flat(t):
            return t[:].rearrange({3: "p a b -> p (a b)", 4: "p a b c -> p (a b c)"}[len(t.shape)])

        for src, dst, ev in views:
            need(act, ev)
            hi = sig("w_hi").on(act.activation(flat(dst[0]), src, ACT.Copy))
            need(dve, ev, hi)
            w_split = sig("w_lo").on(dve.tensor_tensor(flat(dst[1]), src, flat(dst[0]).bitcast(F32), ALU.subtract))

        k = sig("const")
        k.on(pool.memset(ident[:], 0.0))
        k.on(pool.memset(later[:], 0.0))
        k.on(pool.memset(not_later[:], 1.0))
        k.on(pool.memset(lower_e[:], 1.0))
        k.on(pool.memset(minus_half[:], -0.5))
        need(pool, k.on(pool.memset(euler[:], float(np.e))))
        for mask_q, mask_k in zip(mask_qs, mask_ks):
            k.on(pool.memset(mask_q, 1.0))
            need(pool, k.on(pool.memset(mask_k, 0.0)))
        for part in xt:
            for side in (slice(0, HALO), slice(HALO + N, PADDED)):
                k.on(pool.memset(part[:, :, side].bitcast(F32), 0.0))
        iota_i = at("iota_i", [P, NSEL + ST], I32, ring)
        c0 = k.on(pool.iota(iota_i[:, 0:NSEL], pattern=[[1, NSEL]], base=0, channel_multiplier=0))
        c0 = k.on(pool.iota(iota_i[:, NSEL:NSEL + ST], pattern=[[P, ST]], base=0, channel_multiplier=1))
        need(pool, c0)
        k.on(pool.tensor_copy(iota_row[:, :], iota_i[:, 0:NSEL]))
        k.on(pool.tensor_copy(iota_col[:, :], iota_i[:, NSEL:NSEL + ST]))
        k.on(pool.affine_select(out=ident[:, :], in_=ident[:, :], compare_op=ALU.not_equal, fill=1.0,
                                base=0, pattern=[[-1, P]], channel_multiplier=1))
        k.on(pool.affine_select(out=later[:, :], in_=later[:, :], compare_op=ALU.is_ge, fill=1.0,
                                base=0, pattern=[[-1, P]], channel_multiplier=1))
        k.on(pool.affine_select(out=not_later[:, :], in_=not_later[:, :], compare_op=ALU.is_ge, fill=0.0,
                                base=0, pattern=[[-1, P]], channel_multiplier=1))
        c0 = k.on(pool.affine_select(out=lower_e[:, :, :], in_=lower_e[:, :, :], compare_op=ALU.is_ge, fill=0.0,
                                base=-1, pattern=[[1, E], [-1, E]], channel_multiplier=0))
        need(pool, c0)
        for mask_q, mask_k in zip(mask_qs, mask_ks):
            for step, q_base, k_base in ((1, 0, 0), (-1, WIN - 1, 3 * WIN - 1)):
                k.on(pool.affine_select(out=mask_q, in_=mask_q, compare_op=ALU.is_ge, fill=0.0,
                                        base=q_base, pattern=[[step, P]], channel_multiplier=-step * WIN))
                need(pool, k.on(pool.affine_select(out=mask_k, in_=mask_k, compare_op=ALU.is_ge, fill=MASKED,
                                                   base=k_base, pattern=[[0, 3], [step, KEYS]], channel_multiplier=-step * WIN)))
            k.on(pool.memset(mask_k[:, 0, 0:WIN], MASKED))
            need(pool, k.on(pool.memset(mask_k[:, 2, 3 * WIN:KEYS], MASKED)))
        need(pool, w_split)
        for side in (slice(0, HALO), slice(HALO + N, PADDED)):
            consts = k.on(pool.memset(kT[:, :, side], 0.0))

        def ln_stats(srcs, after, key):
            need(dve, *after)
            for j, s in enumerate(srcs):
                e = sig("bn").on(dve.bn_stats(st[:, j, :], s))
            need(dve, e)
            for j in range(len(srcs)):
                e = sig("bn_aggr").on(dve.bn_aggr(mv[:, j, :], st[:, j, :]))
            need(pool, e)
            e = sig("var_eps").on(pool.tensor_scalar(vt[:, :], mv[:, :, 1], LN_EPS, None, ALU.add))
            need(pool, e)
            return sig("rstd").on(pool.tensor_tensor(rs[:, :], vt[:, :], minus_half[:, :], ALU.pow))

        last = {}

        def transposed(g, pr, kind, srcs, ready):
            need(pe, ready, free[TP])
            tp = bview(TP, "p (c n) -> p c n", c=C)
            for j in range(2):
                for c in range(C):
                    ins = pe.transpose(tp[:, c, j * P:(j + 1) * P], srcs[j][:, c * P:(c + 1) * P], ident[:, :])
            e = sig("xpose").on(ins)
            last["y_t"] = e
            col = HALO + (g * TG + pr * 2) * P
            hi, lo = (part[:, :, col:col + 2 * P] for part in xt)
            need(act, e, last.get(("xt", g)), last.get("xf"))
            if kind == "ffn":
                e1 = sig("xt_hi").on(act.activation(hi, tp, ACT.Copy))
                need(dve, e1, last.get(("xt", g)))
                e2 = sig("xt_lo").on(dve.tensor_tensor(lo, tp, hi.bitcast(F32), ALU.subtract))
                free[TP] = e2
                return e2
            for c in range(C):
                e1 = sig("xl_f").on(act.activation(xf_t[:, c, :], tp[:, c, :], ACT.Identity,
                                                   bias=lnb_s[:, c:c + 1], scale=lng_s[:, c:c + 1]))
            free[TP] = e1
            need(pool, e1, last.get(("xt", g)))
            e2 = sig("xl_split").on(pool.tensor_copy(hi, xf_t[:, :, :]))
            need(pool, e2)
            e2 = sig("xl_split").on(pool.tensor_tensor(lo, xf_t[:, :, :], hi.bitcast(F32), ALU.subtract))
            last["xf"] = e2
            return e2

        def ffn_prep(g, src, after, res):
            tiles = [src[:, g * TG + j, :] for j in range(TG)]
            rstd = ln_stats(tiles, after, "ffn")
            yield
            for pr in range(2):
                need(dve, rstd, last.get("y_t"))
                for j in range(2):
                    q = 2 * pr + j
                    e = sig("xn").on(dve.tensor_scalar(y_t[:, q, :], tiles[q], mv[:, q, 0:1], rs[:, q:q + 1],
                                                       ALU.subtract, ALU.mult))
                yield
                xt_ready = transposed(g, pr, "ffn", [y_t[:, 2 * pr + j, :] for j in range(2)], e)
                yield
            res["xt"] = xt_ready
            need(pe, xt_ready, free[MISC])
            lgp = bank[MISC][:, 0:TG * E].rearrange("p (t e) -> p t e", e=E)
            for j in range(TG):
                col = HALO + (g * TG + j) * P
                for c in range(C):
                    ins = mm3(lgp[:, j, :], [w[:, c, col:col + P] for w in xt], [w[:, c, :] for w in rw_s],
                              start=(c == 0), stop=(c == C - 1))
            e = sig("logits").on(ins)
            need(dve, e, last.get("lg"))
            e = free[MISC] = sig("lg").on(dve.tensor_tensor(lg[:, :, :], lgp, rb_s[:, :].unsqueeze(1).broadcast_to([P, TG, E]), ALU.add))
            yield
            need(dve, e)
            sig("lmax").on(dve.tensor_reduce(lmax[:, :], lg[:, :, :], AX_X, ALU.max))
            by_j = lg[:, :, :].unsqueeze(2).broadcast_to([P, TG, E, E])
            by_e = lg[:, :, :].unsqueeze(3).broadcast_to([P, TG, E, E])
            sig("cmp").on(dve.tensor_tensor(cmp_g[:, :, :, :], by_j, by_e, ALU.is_gt))
            e = sig("cmp").on(dve.tensor_tensor(cmp_e[:, :, :, :], by_j, by_e, ALU.is_equal))
            need(dve, e)
            e = sig("cmp").on(dve.tensor_tensor(cmp_e[:, :, :, :], cmp_e[:, :, :, :],
                                                lower_e[:, :, :].unsqueeze(1).broadcast_to([P, TG, E, E]), ALU.mult))
            need(dve, e, (sig("lmax").sem, sig("lmax").n))
            e = sig("cmp").on(dve.tensor_tensor(cmp_g[:, :, :, :], cmp_g[:, :, :, :], cmp_e[:, :, :, :], ALU.add))
            sub = sig("lg").on(dve.tensor_tensor(ex[:, :, :], lg[:, :, :], lmax[:, :].unsqueeze(2).broadcast_to([P, TG, E]), ALU.subtract))
            last["lg"] = sub
            need(pool, sub)
            e2 = sig("exp").on(pool.tensor_tensor(ex[:, :, :].rearrange("p t e -> p (t e)"), euler[:, :],
                                                  ex[:, :, :].rearrange("p t e -> p (t e)"), ALU.pow))
            yield
            need(dve, e)
            e = sig("cmp").on(dve.tensor_reduce(lrank[:, :, :], cmp_g[:, :, :, :], AX_X, ALU.add))
            need(dve, e)
            need(dve, e2)
            e = sig("cmp").on(dve.scalar_tensor_tensor(out=ex[:, :, :], in0=lrank[:, :, :], scalar=TOPK - 0.5,
                                                       in1=ex[:, :, :], op0=ALU.is_lt, op1=ALU.mult))
            need(dve, e)
            e = sig("cmp").on(dve.tensor_reduce(exs[:, :], ex[:, :, :], AX_X, ALU.add))
            need(dve, e)
            e = sig("cmp").on(dve.reciprocal(exs[:, :], exs[:, :]))
            need(dve, e, last.get(("gate", g)))
            gate_ready = sig("gate").on(dve.scalar_tensor_tensor(out=gate[:, g, :, :], in0=ex[:, :, :], scalar=0.5,
                                                                 in1=exs[:, :].unsqueeze(2).broadcast_to([P, TG, E]),
                                                                 op0=ALU.mult, op1=ALU.mult))
            yield
            need(pe, gate_ready, free[MISC])
            for j in range(TG):
                ins = pe.transpose(bank[MISC][0:E, j * P:(j + 1) * P], gate[:, g, j, :], ident[:, :])
            e = sig("gateT").on(ins)
            need(act, e, last.get("gT"))
            free[MISC] = res["gT"] = sig("gT").on(act.activation(gT[:, :, :], bview(MISC, "p (t n) -> p t n", t=TG)[0:E], ACT.Copy))
            res["gate"] = gate_ready

        def advance(gen, n=1):
            for _ in range(n):
                if gen is not None and next(gen, "end") == "end":
                    return

        def finish(gen):
            for _ in gen:
                pass

        def ffn_main(g, src, dst, res, fill, per_step, dst_free=None):
            cols = HALO + g * NG
            hid, hi_used = {}, {}
            acc = {}
            for pr in range(2):
                need(pe, res["gT"], free[MISC])
                for j in range(2):
                    ins = pe.matmul(bank[MISC][:, j * D:(j + 1) * D], gT[:, 2 * pr + j, :], b2_s[:, :], start=True, stop=True)
                e = last["gT"] = sig("bias2").on(ins)
                need(dve, e, dst_free)
                t0 = g * TG + 2 * pr
                e = sig("acc").on(dve.tensor_tensor(dst[:, t0:t0 + 2, :], bview(MISC, "p (t n) -> p t n", t=2),
                                                    src[:, t0:t0 + 2, :], ALU.add))
                free[MISC] = e
                acc[2 * pr] = acc[2 * pr + 1] = e
            for e_ in range(E + 1):
                if e_ < E:
                    b = e_ % 2
                    need(pe, res["xt"], free[b])
                    for c in range(C):
                        ins = mm3(bank[b][:, :], [w[:, c, e_, :] for w in w1_s], [w[:, c, cols:cols + NG] for w in xt],
                                  start=(c == 0), stop=(c == C - 1))
                    h = sig("hidden").on(ins)
                    last[("xt", g)] = h
                    need(act, h, last.get(("hf", b)), last.get(("h", b)))
                    f = free[b] = sig("gelu").on(act.activation(hf[b][:, :], bank[b][:, :], ACT.Gelu, bias=b1_s[:, e_:e_ + 1]))
                    need(act, f)
                    hi = sig("h_hi").on(act.activation(hh[b][:, :], hf[b][:, :], ACT.Copy))
                    need(pool, hi, last.get(("h", b)))
                    hid[e_] = last[("hf", b)] = sig("h_lo").on(pool.tensor_tensor(hl[b][:, :], hf[b][:, :], hh[b][:, :].bitcast(F32), ALU.subtract))
                if e_ >= 1:
                    q = e_ - 1
                    b = q % 2
                    need(pe, hid[q])
                    for pr in range(2):
                        ob = 2 + 2 * b + pr
                        need(pe, free[ob])
                        for j in range(2):
                            cs = slice((2 * pr + j) * P, (2 * pr + j + 1) * P)
                            ins = mm3(bank[ob][:, j * D:(j + 1) * D], [hh[b][:, cs], hl[b][:, cs]], [w[:, q, :] for w in w2_s])
                        oe = sig("expert").on(ins)
                        last[("h", b)] = oe
                        need(dve, oe, res["gate"])
                        for j in range(2):
                            t = 2 * pr + j
                            need(dve, acc[t])
                            xt_ = dst[:, g * TG + t, :]
                            acc[t] = sig("acc").on(dve.scalar_tensor_tensor(
                                out=xt_, in0=bank[ob][:, j * D:(j + 1) * D], scalar=gate[:, g, t, q:q + 1], in1=xt_,
                                op0=ALU.mult, op1=ALU.add))
                        free[ob] = acc[2 * pr + 1]
                advance(fill, per_step)
            last[("gate", g)] = acc[TG - 1]
            return acc[TG - 1]

        def attn_prep(g, after, res):
            tiles = [x1[:, g * TG + j, :] for j in range(TG)]
            rstd = ln_stats(tiles, after, "attn")
            yield
            need(dve, rstd, last.get("y_t"))
            for j in range(TG):
                y = sig("y").on(dve.tensor_scalar(y_t[:, j, :], tiles[j], mv[:, j, 0:1], rs[:, j:j + 1], ALU.subtract, ALU.mult))
            yield
            ys = [y_t[:, j, :] for j in range(TG)]
            rstd = ln_stats(ys, [y], "z")
            e = sig("norm").on(pool.tensor_tensor(rn[:, :], mv[:, :, 0], mv[:, :, 0], ALU.mult))
            need(pool, e)
            e = sig("norm").on(pool.tensor_tensor(rn[:, :], rn[:, :], mv[:, :, 1], ALU.add))
            need(pool, e)
            e = sig("norm").on(pool.tensor_scalar(rn[:, :], rn[:, :], float(D), NORM_MIN ** 2, ALU.mult, ALU.max))
            need(pool, e)
            e = sig("norm").on(pool.tensor_tensor(rn[:, :], rn[:, :], minus_half[:, :], ALU.pow))
            need(pool, e)
            norm = sig("norm").on(pool.tensor_scalar(rn[:, :], rn[:, :], float(D) ** 0.5, None, ALU.mult))
            yield
            junk_w = {}
            for j in range(TG):
                t = g * TG + j
                for r in range(2):
                    need(dve, junk_w.get(r))
                    sc = junk_w[r] = sig("score").on(dve.tensor_tensor_reduce(sjunk[:, r, :], ys[j], rt_s[:, r, :], 1.0, 0.0,
                                                                  ALU.mult, ALU.add, scol[:, r, t:t + 1]))
            res["scores"] = sc
            junk_w.clear()
            yield
            for j in range(TG):
                t = g * TG + j
                need(pool, norm)
                e = sig("yr_hi").on(pool.tensor_scalar(yr[0][:, t, :], ys[j], rn[:, j:j + 1], None, ALU.mult))
                need(dve, e, norm)
                lo = sig("yr_lo").on(dve.scalar_tensor_tensor(out=yr[1][:, t, :], in0=ys[j], scalar=rn[:, j:j + 1],
                                                              in1=yr[0][:, t, :].bitcast(F32), op0=ALU.mult, op1=ALU.subtract))
            res["yr"] = lo
            yield
            for pr in range(2):
                need(dve, rstd, lo, (sig("score").sem, sig("score").n))
                for j in range(2):
                    q = 2 * pr + j
                    e = sig("z").on(dve.tensor_scalar(ys[q], ys[q], mv[:, q, 0:1], rs[:, q:q + 1],
                                                      ALU.subtract, ALU.mult))
                yield
                res["xl"] = transposed(g, pr, "light", [ys[2 * pr + j] for j in range(2)], e)
                yield

        def project_light(g, res, fill):
            cols = HALO + g * NG
            jobs = [("q", ch) for ch in range(HC)] + [("k", ch) for ch in range(HC)]
            jobs += [("v", t) for t in (range(0, TG) if g == 0 else range(TG, T + 1))]
            for n, (kind, ch) in enumerate(jobs):
                b = n % 4
                need(pe, res["xl"], free[b])
                for c in range(C):
                    if kind == "v":
                        w0 = ch * P
                        ins = mm3(bank[b][:, :], [w[:, c, w0:w0 + P] for w in xt],
                                  [w[:, c, 2 * INNER:3 * INNER] for w in wqkv_s], start=(c == 0), stop=(c == C - 1))
                    else:
                        w0 = ch * P + (INNER if kind == "k" else 0)
                        ins = mm3(bank[b][:, :], [w[:, c, w0:w0 + P] for w in wqkv_s],
                                  [w[:, c, cols:cols + NG] for w in xt], start=(c == 0), stop=(c == C - 1))
                e = sig("proj").on(ins)
                last[("xt", 0)] = last[("xt", 1)] = e
                if kind == "q":
                    need(act, e)
                    f = sig("q").on(act.activation(qT[:, ch, g * NG:(g + 1) * NG], bank[b][:, :], ACT.Copy, scale=DH ** -0.5))
                elif kind == "k":
                    need(act, e)
                    f = sig("q").on(act.activation(kT[:, ch, cols:cols + NG], bank[b][:, :], ACT.Copy))
                else:
                    need(act, e)
                    f = sig("q").on(act.activation(V[:, ch, :], bank[b][:, :], ACT.Copy))
                free[b] = f
                res["qkv"] = f
                advance(fill)

        def routing(res):
            for r in range(2):
                for h in range(2):
                    need(pe, res["scores"], free[MISC])
                    for j in range(4):
                        ins = pe.transpose(bank[MISC][:, j * P:(j + 1) * P],
                                           scol[:, r, 4 * h + j:4 * h + j + 1].broadcast_to([P, P]), ident[:, :])
                    e = sig("srow_p").on(ins)
                    need(act, e, last["ring"])
                    row = free[MISC] = sig("srow").on(act.activation(srow[:, r, h * 512:(h + 1) * 512], bank[MISC][:, :], ACT.Copy))
                    yield
            need(dve, row)
            last_z = sig("rank_z").on(dve.memset(rank4[:, :, :, :], 0.0))
            need(dve, last_z)
            done = [last_z, last_z]
            for r in range(2):
                for t in range(T):
                    jk, sj = junk[:, t % 2, :], sjunk[:, t % 2, :]
                    need(dve, done[t % 2])
                    s = scol[:, r, t:t + 1]
                    k4 = rank4[:, r, t, :]
                    d = slice(t * P, (t + 1) * P)
                    if t > 0:
                        sig("rank").on(dve.tensor_scalar(jk[:, 0:t * P], srow[:, r, 0:t * P], s, 0.0, ALU.is_gt, ALU.add, accum_out=k4[:, 0:1]))
                    if t < T - 1:
                        sig("rank").on(dve.tensor_scalar(jk[:, (t + 1) * P:N], srow[:, r, (t + 1) * P:N], s, 0.0, ALU.is_ge, ALU.add, accum_out=k4[:, 1:2]))
                    sig("rank").on(dve.scalar_tensor_tensor(out=sj[:, 0:P], in0=srow[:, r, d], scalar=s, in1=later[:, :],
                                                            op0=ALU.is_ge, op1=ALU.mult, accum_out=k4[:, 2:3]))
                    e = sig("rank").on(dve.scalar_tensor_tensor(out=sj[:, P:2 * P], in0=srow[:, r, d], scalar=s, in1=not_later[:, :],
                                                                op0=ALU.is_gt, op1=ALU.mult, accum_out=k4[:, 3:4]))
                    done[t % 2] = e
                    yield
            need(dve, e)
            res["rank"] = e = sig("rank").on(dve.tensor_reduce(rank[:, :, :], rank4[:, :, :, :], AX_X, ALU.add))
            for h in range(2):
                need(pe, e, free[MISC])
                for j in range(4):
                    ins = pe.transpose(bank[MISC][:, j * P:(j + 1) * P],
                                       rank[:, 0, 4 * h + j:4 * h + j + 1].broadcast_to([P, P]), ident[:, :])
                f = sig("srow_p").on(ins)
                need(act, f)
                free[MISC] = res["rank_row"] = sig("srow").on(act.activation(rank_row[:, h * 512:(h + 1) * 512], bank[MISC][:, :], ACT.Copy))
                yield

        def gather(res):
            oh_used = None
            for r in range(2):
                need(dve, res["rank"], res["x_free"], oh_used)
                for t in range(T):
                    e = sig("onehot").on(dve.tensor_scalar(onehot[:, t, :], iota_row[:, :], rank[:, r, t:t + 1], None, ALU.is_equal))
                b = 4 + r
                need(pe, e, free[b], res["yr"])
                for c in range(C):
                    for t in range(T):
                        for part in range(2):
                            ins = pe.matmul(bank[b][:, c * NSEL:(c + 1) * NSEL], yr[part][:, t, c * P:(c + 1) * P], onehot[:, t, :],
                                            start=(t == 0 and part == 0), stop=(t == T - 1 and part == 1))
                oh_used = sig("gather").on(ins)
                need(act, oh_used, res["proj_done"])
                for c in range(C):
                    f = sig("hin").on(act.activation(hin[r][:, c, :], bank[b][:, c * NSEL:(c + 1) * NSEL], ACT.Copy, scale=gam_s[:, c:c + 1]))
                free[b] = f
                res[f"hin{r}"] = f
            res["x_free"] = oh_used
            need(dve, res["rank_row"], oh_used)
            for kk in range(ST):
                res["rank_hot"] = sig("rank_hot").on(dve.tensor_scalar(rank_hot[:, kk, :], rank_row[:, :], iota_col[:, kk:kk + 1], None, ALU.is_equal))
            n = 0
            for kind in ("q", "k"):
                w, r, dst = (wqh_s, 0, hq) if kind == "q" else (wkvh_s, 1, hk)
                for pr in range(2):
                    b = n % 4
                    need(pe, res[f"hin{r}"], free[b])
                    for j in range(2):
                        ch = 2 * pr + j
                        for c in range(C):
                            ins = pe.matmul(bank[b][:, j * NSEL:(j + 1) * NSEL], w[:, c, ch * P:(ch + 1) * P], hin[r][:, c, :],
                                            start=(c == 0), stop=(c == C - 1))
                    e = sig("hproj").on(ins)
                    need(act, e, res["proj_done"])
                    free[b] = res["hqkv"] = sig("hqkv").on(act.activation(
                        dst[:, 2 * pr:2 * pr + 2, :], bview(b, "p (j n) -> p j n", j=2), ACT.Copy,
                        scale=DH ** -0.5 if kind == "q" else 1.0))
                    n += 1
            for t in range(ST):
                b = n % 4
                need(pe, res["hin1"], free[b])
                for c in range(C):
                    ins = pe.matmul(bank[b][:, :], hin[1][:, c, t * P:(t + 1) * P], wkvh_s[:, c, INNER:2 * INNER],
                                    start=(c == 0), stop=(c == C - 1))
                e = sig("hproj").on(ins)
                need(act, e)
                free[b] = res["hqkv"] = sig("hqkv").on(act.activation(hv[:, t, :], bank[b][:, :], ACT.Copy))
                n += 1

        def attention(tiles, res, tile_done):
            items = [(n, hp) for n in range(len(tiles)) for hp in range(HEADS // 2)]
            soft, turned, pv = {}, {}, {}
            prob_free, probT_free = {}, {}
            normed, o_free, oT_free = None, None, None
            o_ready = {}

            def head(hp, h):
                return hp // 2 * 4 + hp % 2 + 2 * h

            def scores(i):
                nonlocal normed
                n, hp = items[i]
                tl = tiles[n]
                b = i % 2
                need(pe, tl["ready"], free[b])
                sv = bview(b, "p (h k) -> p h k", h=2)
                if tl["mask"] is not None:
                    pe.matmul(sv, mask_qs[hp % 2], mask_ks[hp % 2][:, tl["mask"], :].unsqueeze(1).broadcast_to([2, 2, KEYS]),
                              start=True, stop=False, skip_group_check=True)
                for h in range(2):
                    hs, ch = slice(hp % 2 * DH, (hp % 2 + 1) * DH), head(hp, h) // 2
                    ins = pe.matmul(sv[:, h, :], tl["q"](hs, ch), tl["k"](hs, ch),
                                    start=tl["mask"] is None, stop=True, skip_group_check=True)
                e = sig("sim").on(ins)
                need(dve, e, soft.get(i - 4))
                m = sig("nmax").on(dve.tensor_reduce(nmax[:, i % 4, :], sv, AX_X, ALU.max, negate=True))
                need(act, m, prob_free.get(i - NP), last["ring"])
                if hp == 0:
                    need(act, normed_of.get(n - 2))
                for h in range(2):
                    e = sig("soft").on(act.activation(prob[i % NP][:, h, :], sv[:, h, :], ACT.Exp, bias=nmax[:, i % 4, h:h + 1],
                                                      accum_out=den[:, n % 2, head(hp, h):head(hp, h) + 1]))
                soft[i] = free[b] = e

            normed_of = {}

            def turn(i):
                b = 2 + i % 2
                need(pe, soft[i], free[b])
                for h in range(2):
                    for kk in range(2):
                        ins = pe.transpose(bank[b][:, (2 * h + kk) * P:(2 * h + kk + 1) * P],
                                           prob[i % NP][:, h, kk * P:(kk + 1) * P], ident[:, :])
                e = prob_free[i] = sig("probT_p").on(ins)
                src = bview(b, "p (a n) -> p a n", a=4)
                if i % 2:
                    need(act, e, probT_free.get(i - 2), last["ring"])
                    free[b] = turned[i] = sig("probT_a").on(act.activation(probT[i % 2][:, :, :], src, ACT.Copy))
                else:
                    need(dve, e, probT_free.get(i - 2), last["ring"])
                    free[b] = turned[i] = sig("probT_v").on(dve.tensor_copy(probT[i % 2][:, :, :], src))

            def values(i):
                n, hp = items[i]
                b = 4
                need(pe, turned[i])
                if hp == 0:
                    need(pe, free[b])
                for h in range(2):
                    hd = head(hp, h)
                    for kk in range(2):
                        ins = pe.matmul(bank[b][:, hd * DH:(hd + 1) * DH], probT[i % 2][:, 2 * h + kk, :], tiles[n]["v"](kk, hd),
                                        start=(kk == 0), stop=(kk == 1))
                e = probT_free[i] = sig("pv").on(ins)
                if hp == HEADS // 2 - 1:
                    need(dve, soft[i], last.get("rden"))
                    r = sig("rden").on(dve.reciprocal(rden[:, :], den[:, n % 2, :]))
                    need(dve, e, r, last.get("o_s"), last["ring"])
                    f = sig("o").on(dve.tensor_tensor(o_s[:, :].rearrange("p (h d) -> p h d", h=HEADS),
                                                      bview(b, "p (h d) -> p h d", h=HEADS),
                                                      rden[:, :].unsqueeze(2).broadcast_to([P, HEADS, DH]), ALU.mult))
                    last["rden"] = free[b] = o_ready[n] = normed_of[n] = f

            def out_turn(n):
                need(pe, o_ready[n], free[5])
                for ch in range(HC):
                    ins = pe.transpose(bank[5][:, ch * P:(ch + 1) * P], o_s[:, ch * P:(ch + 1) * P], ident[:, :])
                e = last["o_s"] = sig("oT_p").on(ins)
                need(act, e, last.get("oT_s"), last["ring"])
                f = free[5] = sig("oT").on(act.activation(oT_s[:, :, :], bview(5, "p (c n) -> p c n", c=HC), ACT.Copy))
                return f

            def out_proj(n, f):
                tl = tiles[n]
                need(pe, f, free[5], *tl["extra_ready"])
                ins = None
                for ch in range(HC):
                    ins = pe.matmul(bank[5][:, 0:D], oT_s[:, ch, :], tl["wo"][:, ch, :], start=(ch == 0),
                                    stop=(ch == HC - 1 and not tl["extra"]))
                more = tl["extra"]
                for m, (lh, rh) in enumerate(more):
                    ins = pe.matmul(bank[5][:, 0:D], lh, rh, start=False, stop=(m == len(more) - 1))
                e = last["oT_s"] = sig("y_out").on(ins)
                free[5] = tl["sink"](bank[5][:, 0:D], e)
                tile_done(n, free[5])

            pend = []
            L = len(items)
            for s in range(L + 7):
                if s < L:
                    scores(s)
                if 0 <= s - 2 < L:
                    turn(s - 2)
                if 0 <= s - 3 < L:
                    values(s - 3)
                    if items[s - 3][1] == HEADS // 2 - 1:
                        pend.append((s, items[s - 3][0]))
                if pend and pend[0][0] + 1 == s:
                    oT_ev = out_turn(pend[0][1])
                if pend and pend[0][0] + 2 == s:
                    out_proj(pend.pop(0)[1], oT_ev)
            assert not pend
            return (sig("pv").sem, sig("pv").n)

        def row(b, peeled):
            res = [dict() for _ in range(2)]
            res[0] = first
            prep = ffn_prep(1, xin, [], res[1])
            dst_free = (s_out, None)
            a0 = ffn_main(0, xin, x1, res[0], prep, 2)
            finish(prep)
            ares = {}
            last["ring"] = None
            aprep = attn_prep(0, [a0], ares)
            a1 = ffn_main(1, xin, x1, res[1], aprep, 1)
            finish(aprep)
            ares["x_free"] = a1
            last["ring"] = last[("h", (E - 1) % 2)]
            xl0 = dict(ares)
            aprep = attn_prep(1, [a1], ares)
            advance(aprep, 4)
            project_light(0, xl0, aprep)
            finish(aprep)
            rt = routing(ares)
            project_light(1, ares, rt)
            finish(rt)
            ares["proj_done"] = last[("xt", 0)]
            gather(ares)
            x_free = ares["x_free"]
            if not peeled:
                need(sp, x_free)
                for g in range(G):
                    x_next[g] = sig(f"x_load{g}").on(sp.dma_start(xin[:, g * TG:(g + 1) * TG, :], x_next_src(b, g)), 16)
            last["ring"] = ares["rank_hot"]
            tiles = []
            for n in range(ST):
                def sink(y, e, n=n):
                    need(act, e, ares["rank_hot"])
                    hi = sig("ho_hi").on(act.activation(ho[0][:, n, :], y, ACT.Copy))
                    need(dve, hi)
                    ares["ho"] = sig("ho_lo").on(dve.tensor_tensor(ho[1][:, n, :], y, ho[0][:, n, :].bitcast(F32), ALU.subtract))
                    return ares["ho"]
                tiles.append(dict(
                    ready=ares["hqkv"], mask=None, wo=woh_s, extra=[], extra_ready=[], sink=sink,
                    q=lambda hs, ch, n=n: hq[hs, ch, n * P:(n + 1) * P],
                    k=lambda hs, ch: hk[hs, ch, :],
                    v=lambda kk, hd: hv[:, kk, hd * DH:(hd + 1) * DH]))
            done = attention(tiles, ares, lambda n, e: None)
            last[("xt", 0)] = last[("xt", 1)] = done
            tiles = []
            res2 = [dict() for _ in range(2)]
            summed = {}
            preps = {}
            for t in range(T):
                def sink(y, e, t=t):
                    need(dve, e)
                    summed[t] = sig("x2").on(dve.tensor_tensor(x1[:, t, :], y, x1[:, t, :], ALU.add))
                    return summed[t]
                tiles.append(dict(
                    ready=ares["qkv"], mask=0 if t == 0 else 2 if t == T - 1 else 1, wo=wol_s, sink=sink,
                    extra=[(rank_hot[:, kk, t * P:(t + 1) * P], ho[part][:, kk, :]) for kk in range(ST) for part in range(2)],
                    extra_ready=[ares["ho"], ares["rank_hot"]],
                    q=lambda hs, ch, t=t: qT[hs, ch, t * P:(t + 1) * P],
                    k=lambda hs, ch, t=t: kT[hs, ch, t * P:t * P + KEYS],
                    v=lambda kk, hd, t=t: V[:, t + kk, hd * DH:(hd + 1) * DH]))

            def tile_done(n, e):
                if n == TG - 1:
                    preps[0] = ffn_prep(0, x1, [e], res2[0])
                if n >= TG and n < T - 1:
                    advance(preps[0], 3)
                if n == T - 1:
                    finish(preps[0])
                    preps[1] = ffn_prep(1, x1, [e], res2[1])

            att = attention(tiles, ares, tile_done)
            need(act, att)
            need(pool, att)
            f0 = ffn_main(0, x1, x1, res2[0], preps[1], 2)
            finish(preps[1])
            need(sp, f0)
            store(b, 0)
            nxt = {}
            prep = None if peeled else ffn_prep(0, xin, [x_next[0]], nxt)
            f1 = ffn_main(1, x1, x1, res2[1], prep, 2)
            if prep is not None:
                finish(prep)
            need(sp, f1)
            store(b, 1)
            if not peeled:
                need(dve, x_next[1])
            return nxt

        x_next = {}

        def x_next_src(b, g):
            return x_v[bass.ds(b + 1, 1), :, g * TG:(g + 1) * TG, :].rearrange("b p t d -> p (b t) d")

        def store(b, g):
            gs = slice(g * TG, (g + 1) * TG)
            if isinstance(b, int):
                dst = out_v[b, :, gs, :]
            else:
                dst = out_v[bass.ds(b, 1), :, gs, :].rearrange("b p t d -> p (b t) d")
            sig("store").on(sp.dma_start(dst, x1[:, gs, :]), 16)

        def close_row():
            need(sp, (sig("store").sem, sig("store").n))
            new_counts()

        def new_counts():
            nc.all_engine_barrier()
            for s in sems.values():
                used.add(s.sem)
            pool.sem_clear(clear_range())
            nc.all_engine_barrier()
            for s in sems.values():
                s.n = 0
            waited.clear()
            last.clear()
            for i in range(8):
                free[i] = None

        used = set()

        def clear_range():
            nums = sorted(s.sem.num for s in sems.values())
            assert nums == list(range(nums[0], nums[-1] + 1)), nums
            return range(nums[0], nums[-1] + 1)

        for e_ in (pe, act, dve, pool):
            need(e_, small, w_split, consts)
        first = {}
        finish(ffn_prep(0, xin, [x_ready[0]], first))
        need(dve, x_ready[1])
        names = ("xl_f xl_split norm y score yr_hi yr_lo z hidden gelu h_hi h_lo expert acc bias2 proj q srow_p srow rank_z rank "
                 "onehot gather hin rank_hot hproj hqkv sim nmax soft probT_p probT_a probT_v pv rden o oT_p oT y_out ho_hi ho_lo x2 store").split()
        for n_ in names:
            sig(n_)
        new_counts()
        first = dict.fromkeys(("xt", "gate", "gT"))
        with nc.Fori(0, ROWS - 1) as b:
            row(b, False)
            close_row()
        row(ROWS - 1, True)
        need(sp, (sig("store").sem, sig("store").n))
        nc.all_engine_barrier()


_INS = ["L0_attn_x", "L0_attn_gamma_h", "L0_attn_wq_h", "L0_attn_wkv_h", "L0_attn_wo_h", "L0_attn_ln_g", "L0_attn_ln_b",
        "L0_attn_wqkv_l", "L0_attn_wo_l", "L0_attn_rt_q", "L0_attn_rt_kv", "L0_ffn_router_w", "L0_ffn_router_b",
        "L0_ffn_W1", "L0_ffn_b1", "L0_ffn_W2", "L0_ffn_b2"]


def kernel(**inputs):
    import concourse.bacc as bacc
    from concourse.bass_utils import run_bass_kernel_spmd

    nc = bacc.Bacc("TRN2", target_bir_lowering=False, num_devices=1)
    arrays, args = {}, []
    for name in _INS:
        a = np.ascontiguousarray(inputs[name])
        arrays[f"in_{name}"] = a
        args.append(nc.dram_tensor(f"in_{name}", a.shape, mybir.dt.from_np(a.dtype), kind="ExternalInput").ap())
    shape = arrays["in_L0_attn_x"].shape
    args.append(nc.dram_tensor("out_0", shape, F32, kind="ExternalOutput").ap())
    build(nc, *args)
    r = run_bass_kernel_spmd(nc, [arrays], core_ids=[0])
    return r.results[0]["out_0"]
```

```python
from contextlib import ExitStack
from itertools import chain

import numpy as np

import concourse.bass as bass
from concourse import mybir

F32 = mybir.dt.float32
F32R = mybir.dt.float32r
BF16 = mybir.dt.bfloat16
I32 = mybir.dt.int32
ALU = mybir.AluOpType
ACT = mybir.ActivationFunctionType
AX_X = mybir.AxisListType.X

P = 128
WIN = 64
KEYS = 4 * WIN
HALO = WIN
NSEL = 256
HEADS, DH = 8, 64
TOPK = 2
LN_EPS = 1e-5
NORM_MIN = 1e-12
MASKED = -1e30

PACE = dict(
    ffn1_0=(1, 1, 1, 1, 1, 1, 1, 1, 1, 1),
    ffn1_1=(1, 0, 1, 1, 1, 1, 1, 1, 1, 1),
    ffn2_0=(1, 1, 0, 1, 1, 1, 1, 1, 1, 0),
    ffn2_1=(1, 1, 0, 0, 2, 2, 1, 0, 1, 2),
    project_0=(2, 1, 1, 1, 0, 1, 1, 1, 1, 1, 1, 1),
    project_1=(1, 0, 1, 1, 1, 1, 1, 1, 1, 1, 2, 1, 1),
    attn=(3,),
    routing=(2, 2, 2, 2, 2, 2, 2, 2, 3, 3, 3, 3, 3, 3, 3, 3, 3, 3, 2, 2, 1, 1, 1, 1),
    ffn2_prep=(1, 1, 1, 1, 1, 1, 1, 1, 0, 1, 2, 0, 2, 2, 1, 1, 1, 1, 1, 1, 1, 1, 2, 0),
    bias=(5, 7),
    start=((1, 1), (1, 0), (1, 0), (1, 1), (2, 1), (1, 1), (1, 1)),
)


class Signal:

    def __init__(self, sem):
        self.sem, self.n = sem, 0

    def on(self, ins, by=1):
        ins.then_inc(self.sem, by)
        self.n += by
        return self.sem, self.n


def build(nc, x_in, gamma_h, wq_h, wkv_h, wo_h, ln_g, ln_b, wqkv, wo_l, rt_q, rt_kv,
          router_w, router_b, w1, b1, w2, b2, out):
    pe, act, dve, pool, sp = nc.tensor, nc.scalar, nc.vector, nc.gpsimd, nc.sync
    ROWS, N, D = x_in.shape
    E, _, FF = w1.shape
    T = N // P
    C = D // P
    INNER = HEADS * DH
    HC = INNER // P
    G = 2
    TG = T // G
    NG = TG * P
    ST = NSEL // P
    PADDED = N + 2 * HALO
    BIAS_AT = tuple(PACE["bias"])
    assert FF == P and KEYS == NSEL and HC == 4 and TG == 4

    ctx = ExitStack()
    with ctx:
        sems = {}

        def sig(name):
            if name not in sems:
                sems[name] = Signal(ctx.enter_context(nc.semaphore(name)))
            return sems[name]

        def need(eng, *events):
            for e in events:
                if e is None:
                    continue
                key = (str(eng.engine), str(e[0]))
                if waited.get(key, 0) < e[1]:
                    waited[key] = e[1]
                    eng.wait_ge(*e)

        waited = {}

        top = [-(-nc.sbuf_base // 64) * 64]

        def place(nbytes):
            at = top[0]
            top[0] += -(-nbytes // 64) * 64
            assert top[0] <= nc.sbuf_usable_end, top[0]
            return at

        def at(name, shape, dt, offset):
            return nc.alloc_sbuf_tensor_at(name, shape, dt, offset=offset)

        def sb(name, shape, dt=F32):
            size = int(np.prod(shape[1:])) * (2 if dt == BF16 else 4)
            return at(name, shape, dt, place(size))

        def pair(name, shape):
            return sb(name + "_hi", shape, F32R), sb(name + "_lo", shape, F32R)

        w1_s = pair("w1", [P, C, E, FF])
        w2_s = pair("w2", [P, E, D])
        wqkv_s = pair("wqkv", [P, C, 3 * INNER])
        rw_s = sb("rw", [P, C, 2, E], F32R)
        wqh_s = sb("wqh", [P, C, INNER])
        wkvh_s = sb("wkvh", [P, C, 2 * INNER])
        wol_s = sb("wol", [P, HC, D])
        woh_s = sb("woh", [P, HC, D])
        b2_s = sb("b2s", [64 + E, D], F32R)
        b1_s = sb("b1s", [P, E])
        rb_s = sb("rbs", [P, E])
        gam_s = sb("gams", [P, C])
        lng_s = sb("lngs", [P, C])
        lnb_s = sb("lnbs", [P, C])
        rt_s = sb("rts", [P, 2, D])
        ident = sb("ident", [P, P])
        iota_row = sb("iota_row", [P, NSEL])
        iota_col = sb("iota_col", [P, ST])
        later = sb("later", [P, P], BF16)
        not_later = sb("not_later", [P, P], BF16)
        lower_e = sb("lower_e", [P, E, E], BF16)
        minus_half = sb("minus_half", [P, TG])
        euler = sb("euler", [P, TG])
        gT = sb("gT", [64 + E, TG, P], F32R)
        mask = sb("mask", [P, 3, KEYS], BF16)

        x_off = place(N * D // P * 4)
        xin = at("xin", [P, T, D], F32, x_off)
        srow = at("srow", [P, 2, N], F32, x_off)
        onehot_kv = at("onehot_kv", [P, T, NSEL], F32R, x_off)
        x1 = sb("x1", [P, T, D])
        yr_off = place(2 * T * D * 4)
        yr = (at("yr_hi", [P, T, D], F32R, yr_off), at("yr_lo", [P, T, D], F32R, yr_off + T * D * 4))
        rank_hot = at("rank_hot", [P, ST, N], F32R, yr_off)
        ho = (at("ho_hi", [P, ST, D], F32R, yr_off + ST * N * 4),
              at("ho_lo", [P, ST, D], F32R, yr_off + ST * N * 4 + ST * D * 4))
        xt_off = place(2 * C * PADDED * 4)
        xt = (at("xt_hi", [P, C, PADDED], F32R, xt_off),
              at("xt_lo", [P, C, PADDED], F32R, xt_off + C * PADDED * 4))
        q_off = top[0]
        qT = sb("qT", [P, HC, N])
        kT = sb("kT", [P, HC, PADDED])
        V = sb("V", [P, T + 1, INNER])
        half = HALO * 4
        onehot_q = [at(f"onehot_q{n}", [P, T // 2, NSEL], F32R, xt_off + half + n * PADDED * 4) for n in range(2)]
        onehots = [[onehot_q[t // (T // 2)][:, t % (T // 2), :] for t in range(T)], [onehot_kv[:, t, :] for t in range(T)]]
        hin = [at(f"hin{r}", [P, C, NSEL], F32, xt_off + half + r * C * NSEL * 4) for r in range(2)]
        hq = at("hq", [P, HC, NSEL], F32, xt_off + half + PADDED * 4)
        hk = at("hk", [P, HC, NSEL], F32, xt_off + half + 2 * PADDED * 4)
        hv = at("hv", [P, ST, INNER], F32, xt_off + half + 3 * PADDED * 4)
        NP = 3
        ring = place((NP * 2 * KEYS + 2 * 4 * P + 2 * INNER) * 4)
        NH = 3
        hf = [at(f"hf{i}", [P, NG], F32, ring + i * NG * 4) for i in range(NH)]
        hl = [at(f"hl{i}", [P, NG], F32R, ring + i * NG * 4) for i in range(NH)]
        hh = [at(f"hh{i}", [P, NG], F32R, ring + (NH + i) * NG * 4) for i in range(NH)]
        prob = [at(f"prob{i}", [P, 2, KEYS], F32, ring + i * 2 * KEYS * 4) for i in range(NP)]
        probT = [at(f"probT{i}", [P, 4, P], F32, ring + (NP * 2 * KEYS + i * 4 * P) * 4) for i in range(2)]
        o_s = at("o_s", [P, INNER], F32, ring + (NP * 2 * KEYS + 8 * P) * 4)
        oT_s = at("oT_s", [P, HC, P], F32, ring + (NP * 2 * KEYS + 8 * P + INNER) * 4)
        y_off = place(TG * D * 4)
        y_t = at("y_t", [P, TG, D], F32, y_off)
        junk = at("junk", [P, 2, N], mybir.dt.uint8, y_off)
        sjunk = at("sjunk", [P, 2, D], mybir.dt.uint8, y_off + 2 * N)
        rank_row = at("rank_row", [P, N], F32, y_off)
        cmp_g = at("cmp_g", [P, TG, E, E], BF16, y_off)
        cmp_e = at("cmp_e", [P, TG, E, E], BF16, y_off + TG * E * E * 2)
        xf_t = at("xf_t", [P, C, 2 * P], F32, ring + 6 * NG * 4)
        st = sb("st", [P, TG, 6])
        mv = sb("mv", [P, TG, 2])
        vt = sb("vt", [P, TG])
        rs = sb("rs", [P, TG])
        rn = sb("rn", [P, TG])
        nm = sb("nm", [P, TG])
        scol = sb("scol", [P, 2, T])
        rank4 = sb("rank4", [P, 2, T, 4])
        rank = sb("rank", [P, 2, T])
        lg = sb("lg", [P, TG, E])
        lmax = sb("lmax", [P, TG])
        lrank = sb("lrank", [P, TG, E])
        l2nd = sb("l2nd", [P, TG, E])
        wt = sb("wt", [P, 2, TG])
        place_1 = sb("place_1", [P, TG, E])
        t2nd = sb("t2nd", [P, TG])
        gate = sb("gate", [P, G, TG, E])
        nmax = sb("nmax", [P, 4, 2])
        den = sb("den", [P, 2, HEADS])
        rden = sb("rden", [P, HEADS])

        bank = [ctx.enter_context(nc.psum_tensor(f"bank{i}", [P, 512], F32)) for i in range(8)]
        free = [None] * 8
        TP, MISC = 6, 7

        def bview(i, pattern, **kw):
            return bank[i][:, :].rearrange(pattern, **kw)

        def mm3(o, w, x, start=True, stop=True):
            pe.matmul(o, w[0], x[0], start=start, stop=False)
            pe.matmul(o, w[1], x[0], start=False, stop=False)
            return pe.matmul(o, w[0], x[1], start=False, stop=stop)

        def bcast_rows(v, n):
            return v.rearrange("(a n) -> a n", a=1).broadcast_to([P, n])

        b2_f = at("b2_f", [E, D], F32, ring + 4096)
        wst = at("wst", [P, 2 * P * C * E + C * 3 * INNER + C * E], F32, q_off)
        loads = [
            (lambda o: o.rearrange("p (c n) -> p c n", c=C), router_w.rearrange("(c p) n -> p c n", p=P), [rw_s[:, :, n, :] for n in range(2)], C * E),
            (lambda o: o.rearrange("p (c e f) -> p c e f", c=C, e=E), w1.rearrange("e (c p) f -> p c e f", p=P), w1_s, C * E * FF),
            (lambda o: o.rearrange("p (e n) -> p e n", e=E), w2.rearrange("e p n -> p e n"), w2_s, E * D),
            (lambda o: o.rearrange("p (c n) -> p c n", c=C), wqkv.rearrange("(c p) n -> p c n", p=P), wqkv_s, C * 3 * INNER),
        ]
        late_loaded = ctx.enter_context(nc.semaphore("late_loaded"))
        stored = [ctx.enter_context(nc.semaphore(f"stored{g}")) for g in range(G)]
        for s_ in stored:
            sp.sem_inc(s_, 16)
        x_v = x_in.rearrange("b (t p) d -> b p t d", p=P)
        out_v = out.rearrange("b (t p) d -> b p t d", p=P)

        x_ready = {}

        def load_first(g):
            x_ready[g] = sig(f"x_load{g}").on(sp.dma_start(xin[:, g * TG:(g + 1) * TG, :], x_v[0, :, g * TG:(g + 1) * TG, :]), 16)

        load_first(0)
        o = 0
        views = []
        for shape, src, dst, n in loads:
            v = shape(wst[:, o:o + n])
            for c in range(src.shape[1]):
                ev = sig(f"w_load{len(views)}").on(sp.dma_start(v[:, c], src[:, c]), 16)
            views.append((wst[:, o:o + n], dst, ev))
            o += n
            if dst is w1_s:
                load_first(1)
        for dst, src in ((rb_s[:, :], bcast_rows(router_b, E)), (b1_s[:, :], b1.rearrange("e f -> f e"))):
            bias_loaded = sig("bias_load").on(act.dma_start(dst, src, allow_slow_non_contiguous=True), 16)
        for dst, src in ((b2_f[:, :], b2), (gam_s[:, :], gamma_h.rearrange("(c p) -> p c", p=P)),
                         (lng_s[:, :], ln_g.rearrange("(c p) -> p c", p=P)), (lnb_s[:, :], ln_b.rearrange("(c p) -> p c", p=P)),
                         (rt_s[:, 0, :], bcast_rows(rt_q, D)), (rt_s[:, 1, :], bcast_rows(rt_kv, D))):
            small = sig("c_load").on(sp.dma_start(dst, src, allow_slow_non_contiguous=True), 16)
        late = 0
        for dst, src in ((wqh_s[:, :, :], wq_h.rearrange("(c p) n -> p c n", p=P)),
                         (wkvh_s[:, :, :], wkv_h.rearrange("(c p) n -> p c n", p=P)),
                         (wol_s[:, :, :], wo_l.rearrange("(c p) n -> p c n", p=P)),
                         (woh_s[:, :, :], wo_h.rearrange("(c p) n -> p c n", p=P))):
            sp.dma_start(dst, src).then_inc(late_loaded, 16)
            late += 16

        def flat(t):
            if t.shape[-1] == E:
                return t
            return t[:].rearrange({3: "p a b -> p (a b)", 4: "p a b c -> p (a b c)"}[len(t.shape)])

        def split_weights():
            for src, dst, ev in views:
                if dst[0].shape[-1] == E:
                    src = src.rearrange("p (c n) -> p c n", c=C)
                need(act, ev)
                hi = sig("w_hi").on(act.activation(flat(dst[0]), src, ACT.Copy))
                need(dve, ev, hi)
                res_w["split"] = sig("w_lo").on(dve.tensor_tensor(flat(dst[1]), src, flat(dst[0]).bitcast(F32), ALU.subtract))
                yield
            need(act, small, b2_zero)
            for at_ in (0, 32):
                hi = sig("w_hi").on(act.activation(b2_s[at_:at_ + E, :], b2_f[:, :], ACT.Copy))
            need(dve, hi)
            sig("w_lo").on(dve.tensor_tensor(b2_s[64:64 + E, :], b2_f[:, :], b2_s[0:E, :].bitcast(F32), ALU.subtract))
            yield

        res_w = {}

        k = sig("const")
        need(pool, k.on(pool.memset(gT[:].bitcast(F32), 0.0)))
        b2_zero = k.on(pool.memset(b2_s[:].bitcast(F32), 0.0))
        need(pool, b2_zero)
        k.on(pool.memset(ident[:], 0.0))
        k.on(pool.memset(later[:], 0.0))
        k.on(pool.memset(not_later[:], 1.0))
        k.on(pool.memset(lower_e[:], 1.0))
        k.on(pool.memset(minus_half[:], -0.5))
        k.on(pool.memset(euler[:], float(np.e)))
        k.on(pool.memset(mask[:], 0.0))
        for part in xt:
            for side in (slice(0, HALO), slice(HALO + N, PADDED)):
                k.on(pool.memset(part[:, :, side].bitcast(F32), 0.0))
        iota_i = at("iota_i", [P, NSEL + ST], I32, ring)
        c0 = k.on(pool.iota(iota_i[:, 0:NSEL], pattern=[[1, NSEL]], base=0, channel_multiplier=0))
        c0 = k.on(pool.iota(iota_i[:, NSEL:NSEL + ST], pattern=[[P, ST]], base=0, channel_multiplier=1))
        need(pool, c0)
        k.on(pool.tensor_copy(iota_row[:, :], iota_i[:, 0:NSEL]))
        k.on(pool.tensor_copy(iota_col[:, :], iota_i[:, NSEL:NSEL + ST]))
        k.on(pool.affine_select(out=ident[:, :], in_=ident[:, :], compare_op=ALU.not_equal, fill=1.0,
                                base=0, pattern=[[-1, P]], channel_multiplier=1))
        k.on(pool.affine_select(out=later[:, :], in_=later[:, :], compare_op=ALU.is_ge, fill=1.0,
                                base=0, pattern=[[-1, P]], channel_multiplier=1))
        k.on(pool.affine_select(out=not_later[:, :], in_=not_later[:, :], compare_op=ALU.is_ge, fill=0.0,
                                base=0, pattern=[[-1, P]], channel_multiplier=1))
        c0 = k.on(pool.affine_select(out=lower_e[:, :, :], in_=lower_e[:, :, :], compare_op=ALU.is_ge, fill=0.0,
                                base=-1, pattern=[[1, E], [-1, E]], channel_multiplier=0))
        need(pool, c0)
        for w in range(2):
            rows_w = slice(w * WIN, (w + 1) * WIN)
            dead = slice(3 * WIN, KEYS) if w == 0 else slice(0, WIN)
            k.on(pool.memset(mask[rows_w, :, dead], MASKED))
        k.on(pool.memset(mask[WIN:P, 2, 3 * WIN:KEYS], MASKED))
        consts = k.on(pool.memset(mask[0:WIN, 0, 0:WIN], MASKED))

        def ln_stats(srcs, after, key):
            need(dve, *after)
            for j, s in enumerate(srcs):
                e = sig("bn").on(dve.bn_stats(st[:, j, :], s))
            need(dve, e)
            for j in range(len(srcs)):
                e = sig("bn_aggr").on(dve.bn_aggr(mv[:, j, :], st[:, j, :]))
            need(pool, e)
            e = sig("var_eps").on(pool.tensor_scalar(vt[:, :], mv[:, :, 1], LN_EPS, None, ALU.add))
            m = sig("var_eps").on(pool.tensor_scalar(nm[:, :], mv[:, :, 0], -1.0, None, ALU.mult))
            need(pool, e)
            e = sig("rstd").on(pool.tensor_tensor(rs[:, :], vt[:, :], minus_half[:, :], ALU.pow))
            need(pool, e, m)
            return sig("rstd").on(pool.tensor_tensor(nm[:, :], nm[:, :], rs[:, :], ALU.mult))

        def normalise(dst, src, q):
            return sig("norm_a").on(act.activation(dst, src, ACT.Identity, bias=nm[:, q:q + 1], scale=rs[:, q:q + 1]))

        last = {}
        in_use = {"gT": False}

        def transposed(g, pr, kind, srcs, ready):
            tb = (TP, MISC)[pr]
            need(pe, ready, free[tb])
            tp = bview(tb, "p (c n) -> p c n", c=C)
            for j in range(2):
                for c in range(C):
                    ins = pe.transpose(tp[:, c, j * P:(j + 1) * P], srcs[j][:, c * P:(c + 1) * P], ident[:, :])
            e = sig("xpose").on(ins)
            last["y_t"] = e
            col = HALO + (g * TG + pr * 2) * P
            hi, lo = (part[:, :, col:col + 2 * P] for part in xt)
            need(act, e, last.get(("xt", g)), last.get("xf"))
            if kind == "ffn":
                e1 = sig("xt_hi").on(act.activation(hi, tp, ACT.Copy))
                need(dve, e1, last.get(("xt", g)))
                e2 = sig("xt_lo").on(dve.tensor_tensor(lo, tp, hi.bitcast(F32), ALU.subtract))
                free[tb] = e2
                return e2
            for c in range(C):
                for dst in (hi, xf_t):
                    e1 = sig("xl_f").on(act.activation(dst[:, c, :], tp[:, c, :], ACT.Identity,
                                                       bias=lnb_s[:, c:c + 1], scale=lng_s[:, c:c + 1]))
            free[tb] = e1
            need(pool, e1, last.get(("xt", g)))
            e2 = sig("xl_lo").on(pool.tensor_tensor(lo, xf_t[:, :, :], hi.bitcast(F32), ALU.subtract))
            last["xf"] = e2
            return e2

        def ffn_prep(g, src, after, res):
            tiles = [src[:, g * TG + j, :] for j in range(TG)]
            rstd = ln_stats(tiles, after, "ffn")
            yield
            need(act, rstd, last.get("y_t"))
            for q in range(TG):
                e = normalise(y_t[:, q, :], tiles[q], q)
            yield
            for pr in range(2):
                xt_ready = transposed(g, pr, "ffn", [y_t[:, 2 * pr + j, :] for j in range(2)], e)
                if pr == 0:
                    yield
            res["xt"] = xt_ready
            yield
            need(pe, xt_ready, free[TP])
            lgp = bank[TP][:, 0:TG * 2 * E].rearrange("p (t w e) -> p t w e", w=2, e=E)
            for j in range(TG):
                col = HALO + (g * TG + j) * P
                for c in range(C):
                    for n, part in enumerate(xt):
                        ins = pe.matmul(lgp[:, j, :, :], part[:, c, col:col + P], rw_s[:, c, :, :],
                                        start=(c == 0 and n == 0), stop=(c == C - 1 and n == 1))
            e = sig("logits").on(ins)
            need(dve, e, last.get("lg"))
            e = sig("lg").on(dve.tensor_tensor(lg[:, :, :], lgp[:, :, 0, :], rb_s[:, :].unsqueeze(1).broadcast_to([P, TG, E]), ALU.add))
            need(dve, e)
            e = free[TP] = sig("lg").on(dve.tensor_tensor(lg[:, :, :], lgp[:, :, 1, :], lg[:, :, :], ALU.add))
            yield
            need(dve, e)
            sig("lmax").on(dve.tensor_reduce(lmax[:, :], lg[:, :, :], AX_X, ALU.max))
            by_j = lg[:, :, :].unsqueeze(2).broadcast_to([P, TG, E, E])
            by_e = lg[:, :, :].unsqueeze(3).broadcast_to([P, TG, E, E])
            sig("cmp").on(dve.tensor_tensor(cmp_g[:, :, :, :], by_j, by_e, ALU.is_gt))
            e = sig("cmp").on(dve.tensor_tensor(cmp_e[:, :, :, :], by_j, by_e, ALU.is_equal))
            need(dve, e)
            e = sig("cmp").on(dve.tensor_tensor(cmp_e[:, :, :, :], cmp_e[:, :, :, :],
                                                lower_e[:, :, :].unsqueeze(1).broadcast_to([P, TG, E, E]), ALU.mult))
            need(dve, e, (sig("lmax").sem, sig("lmax").n))
            e = sig("cmp").on(dve.tensor_tensor(cmp_g[:, :, :, :], cmp_g[:, :, :, :], cmp_e[:, :, :, :], ALU.add))
            need(dve, e)
            last["lg"] = last["y_t"] = e = sig("cmp").on(dve.tensor_reduce(lrank[:, :, :], cmp_g[:, :, :, :], AX_X, ALU.add))
            yield
            need(dve, e)
            e = last["lg"] = sig("cmp").on(dve.scalar_tensor_tensor(out=l2nd[:, :, :], in0=lrank[:, :, :], scalar=1.0,
                                                                    in1=lg[:, :, :], op0=ALU.is_equal, op1=ALU.mult))
            need(dve, e)
            e = sig("cmp").on(dve.tensor_reduce(t2nd[:, :], l2nd[:, :, :], AX_X, ALU.add))
            need(dve, e)
            e = sig("cmp").on(dve.tensor_tensor(t2nd[:, :], t2nd[:, :], lmax[:, :], ALU.subtract))
            need(pool, e)
            e = sig("exp").on(pool.tensor_tensor(t2nd[:, :], euler[:, :], t2nd[:, :], ALU.pow))
            yield
            need(dve, e)
            e = sig("cmp").on(dve.tensor_scalar(wt[:, 0, :], t2nd[:, :], 1.0, 2.0, ALU.add, ALU.mult))
            need(dve, e)
            e = sig("cmp").on(dve.reciprocal(wt[:, 0, :], wt[:, 0, :]))
            need(dve, e)
            e = sig("cmp").on(dve.tensor_tensor(wt[:, 1, :], t2nd[:, :], wt[:, 0, :], ALU.mult))
            need(dve, e)
            w_of = [wt[:, n, :].unsqueeze(2).broadcast_to([P, TG, E]) for n in range(2)]
            need(dve, last.get(("gate", g)))
            sig("cmp").on(dve.scalar_tensor_tensor(out=place_1[:, :, :], in0=lrank[:, :, :], scalar=1.0, in1=w_of[1],
                                                   op0=ALU.is_equal, op1=ALU.mult))
            e = sig("cmp").on(dve.scalar_tensor_tensor(out=gate[:, g, :, :], in0=lrank[:, :, :], scalar=0.0, in1=w_of[0],
                                                       op0=ALU.is_equal, op1=ALU.mult))
            need(dve, e)
            gate_ready = sig("gate").on(dve.tensor_tensor(gate[:, g, :, :], gate[:, g, :, :], place_1[:, :, :], ALU.add))
            res["gate"] = gate_ready
            yield
            while in_use["gT"]:
                yield
            in_use["gT"] = True
            need(pe, gate_ready, free[MISC])
            for j in range(TG):
                ins = pe.transpose(bank[MISC][0:E, j * P:(j + 1) * P], gate[:, g, j, :], ident[:, :])
            e = sig("gateT").on(ins)
            need(act, e, last.get("gT"))
            gp = bview(MISC, "p (t n) -> p t n", t=TG)[0:E]
            for at_ in (0, 64):
                e = sig("gT_hi").on(act.activation(gT[at_:at_ + E, :, :], gp, ACT.Copy))
            need(dve, e, last.get("gT"))
            free[MISC] = res["gT"] = sig("gT").on(dve.tensor_tensor(gT[32:32 + E, :, :], gp, gT[0:E, :, :].bitcast(F32), ALU.subtract))

        def advance(gen, n=1):
            for _ in range(n):
                if gen is not None and next(gen, "end") == "end":
                    return

        def until(gen, res, key):
            while key not in res:
                advance(gen)

        def finish(gen):
            for _ in gen:
                pass

        def ffn_main(g, src, dst, res, fill, pace, stored_before=None):
            cols = HALO + g * NG
            hid, hi_used = {}, {}
            acc = {}
            for s_ in range(E + 2):
                if s_ < E:
                    b, r = s_ % 2, s_ % NH
                    need(pe, res["xt"], free[b])
                    for c in range(C):
                        ins = mm3(bank[b][:, :], [w[:, c, s_, :] for w in w1_s], [w[:, c, cols:cols + NG] for w in xt],
                                  start=(c == 0), stop=(c == C - 1))
                    h = sig("hidden").on(ins)
                    last[("xt", g)] = h
                    need(act, h, last.get(("h", r)))
                    for dst_h in (hf[r], hh[r]):
                        f = free[b] = sig("gelu").on(act.activation(dst_h[:, :], bank[b][:, :], ACT.Gelu, bias=b1_s[:, s_:s_ + 1]))
                    need(pool, f)
                    hid[s_] = sig("h_lo").on(pool.tensor_tensor(hl[r][:, :], hf[r][:, :], hh[r][:, :].bitcast(F32), ALU.subtract))
                if s_ >= 2:
                    q = s_ - 2
                    until(fill, res, "gate")
                    if q == 0 and stored_before is not None:
                        dve.wait_ge(stored[g], stored_before)
                    b, r = q % 2, q % NH
                    need(pe, hid[q])
                    for pr in range(2):
                        ob = 2 + 2 * b + pr
                        need(pe, free[ob])
                        for j in range(2):
                            cs = slice((2 * pr + j) * P, (2 * pr + j + 1) * P)
                            ins = mm3(bank[ob][:, j * D:(j + 1) * D], [hh[r][:, cs], hl[r][:, cs]], [w[:, q, :] for w in w2_s])
                        oe = sig("expert").on(ins)
                        last[("h", r)] = oe
                        need(dve, oe, res["gate"])
                        for j in range(2):
                            t = 2 * pr + j
                            need(dve, acc.get(t))
                            xt_, at_ = dst[:, g * TG + t, :], src[:, g * TG + t, :]
                            acc[t] = sig("acc").on(dve.scalar_tensor_tensor(
                                out=xt_, in0=bank[ob][:, j * D:(j + 1) * D], scalar=gate[:, g, t, q:q + 1],
                                in1=at_ if q == 0 else xt_,
                                op0=ALU.mult, op1=ALU.add))
                        free[ob] = acc[2 * pr + 1]
                if s_ in BIAS_AT:
                    until(fill, res, "gT")
                    pr = BIAS_AT.index(s_)
                    need(pe, res["gT"], free[MISC])
                    for j in range(2):
                        ins = pe.matmul(bank[MISC][:, j * D:(j + 1) * D], gT[:, 2 * pr + j, :], b2_s[:, :], start=True, stop=True)
                    e = last["gT"] = sig("bias2").on(ins)
                    in_use["gT"] = pr == 0
                    need(dve, e, acc[2 * pr + 1])
                    here = dst[:, g * TG + 2 * pr:g * TG + 2 * pr + 2, :]
                    acc[2 * pr] = acc[2 * pr + 1] = free[MISC] = sig("acc").on(dve.tensor_tensor(
                        here, bview(MISC, "p (t n) -> p t n", t=2), here, ALU.add))
                advance(fill, PACE[pace][s_])
            last[("gate", g)] = acc[TG - 1]
            return acc[TG - 1]

        z_t = at("z_t", [P, TG, D], F32, ring)

        def attn_prep(g, after, res):
            tiles = [x1[:, g * TG + j, :] for j in range(TG)]
            rstd = ln_stats(tiles, after, "attn")
            yield
            need(act, rstd, last.get("y_t"), *after)
            for j in range(TG):
                y = normalise(y_t[:, j, :], tiles[j], j)
            yield
            ys = [y_t[:, j, :] for j in range(TG)]
            rstd = ln_stats(ys, [y], "z")
            e = sig("norm").on(pool.tensor_tensor(rn[:, :], mv[:, :, 0], mv[:, :, 0], ALU.mult))
            need(pool, e)
            e = sig("norm").on(pool.tensor_tensor(rn[:, :], rn[:, :], mv[:, :, 1], ALU.add))
            need(pool, e)
            e = sig("norm").on(pool.tensor_scalar(rn[:, :], rn[:, :], float(D), NORM_MIN ** 2, ALU.mult, ALU.max))
            need(pool, e)
            e = sig("norm").on(pool.tensor_tensor(rn[:, :], rn[:, :], minus_half[:, :], ALU.pow))
            need(pool, e)
            norm = sig("norm").on(pool.tensor_scalar(rn[:, :], rn[:, :], float(D) ** 0.5, None, ALU.mult))
            yield
            def scores_and_parts():
                for j in range(TG):
                    t = g * TG + j
                    for r in range(2):
                        sc = sig("score").on(dve.tensor_tensor_reduce(yr[r][:, t, :], ys[j], rt_s[:, r, :], 1.0, 0.0,
                                                                      ALU.mult, ALU.add, scol[:, r, t:t + 1]))
                res["scores"] = sc
                yield
                for j in range(TG):
                    need(act, norm, sc)
                    hi = sig("yr_hi").on(act.activation(yr[0][:, g * TG + j, :], ys[j], ACT.Copy, scale=rn[:, j:j + 1]))
                yield
                need(dve, hi, norm)
                for j in range(TG):
                    t = g * TG + j
                    lo = sig("yr_lo").on(dve.scalar_tensor_tensor(out=yr[1][:, t, :], in0=ys[j], scalar=rn[:, j:j + 1],
                                                                  in1=yr[0][:, t, :].bitcast(F32), op0=ALU.mult, op1=ALU.subtract))
                res["yr"] = lo
                yield

            def z_tiles(zs, *after):
                need(act, rstd, y, *after)
                for q in range(TG):
                    res["z"] = normalise(zs[q], ys[q], q)

            def turn_z(zs, pr):
                res["xl"] = transposed(g, pr, "light", zs[2 * pr:2 * pr + 2], res["z"])

            if g == 0:
                yield from scores_and_parts()
                z_tiles(ys, res["yr"], res["scores"])
                yield
                yield
                turn_z(ys, 0)
                yield
                turn_z(ys, 1)
                yield
            else:
                zs = [z_t[:, j, :] for j in range(TG)]
                z_tiles(zs, last["ring"])
                yield
                for n, _ in enumerate(scores_and_parts()):
                    yield
                    if n == 1:
                        yield
                        turn_z(zs, 0)
                        yield
                turn_z(zs, 1)
                yield
                last["y_t"] = res["yr"]

        def project_light(g, res, banks):
            cols = HALO + g * NG
            jobs = [("q", ch) for ch in range(HC)] + [("k", ch) for ch in range(HC)]
            jobs += [("v", t) for t in (range(0, TG) if g == 0 else range(TG, T + 1))]
            for n, (kind, ch) in enumerate(jobs):
                b = banks[n % len(banks)]
                need(pe, res["xl"], free[b])
                for c in range(C):
                    if kind == "v":
                        w0 = ch * P
                        ins = mm3(bank[b][:, :], [w[:, c, w0:w0 + P] for w in xt],
                                  [w[:, c, 2 * INNER:3 * INNER] for w in wqkv_s], start=(c == 0), stop=(c == C - 1))
                    else:
                        w0 = ch * P + (INNER if kind == "k" else 0)
                        ins = mm3(bank[b][:, :], [w[:, c, w0:w0 + P] for w in wqkv_s],
                                  [w[:, c, cols:cols + NG] for w in xt], start=(c == 0), stop=(c == C - 1))
                e = sig("proj").on(ins)
                last[("xt", 0)] = last[("xt", 1)] = e
                if kind == "q":
                    need(act, e)
                    f = sig("q").on(act.activation(qT[:, ch, g * NG:(g + 1) * NG], bank[b][:, :], ACT.Copy, scale=DH ** -0.5))
                elif kind == "k":
                    need(act, e)
                    f = sig("q").on(act.activation(kT[:, ch, cols:cols + NG], bank[b][:, :], ACT.Copy))
                else:
                    need(act, e)
                    f = sig("q").on(act.activation(V[:, ch, :], bank[b][:, :], ACT.Copy))
                free[b] = f
                res["qkv"] = f
                yield
            res["proj_done"] = e

        def routing(res):
            res["scores_done"] = True
            for r in range(2):
                for h in range(2):
                    need(pe, res["scores"], free[MISC])
                    for j in range(4):
                        ins = pe.transpose(bank[MISC][:, j * P:(j + 1) * P],
                                           scol[:, r, 4 * h + j:4 * h + j + 1].broadcast_to([P, P]), ident[:, :])
                    e = sig("srow_p").on(ins)
                    need(act, e, res["a1"])
                    row = free[MISC] = sig("srow").on(act.activation(srow[:, r, h * 512:(h + 1) * 512], bank[MISC][:, :], ACT.Copy))
                    yield
            need(dve, row)
            need(dve, res["z"], res["yr"])
            last_z = sig("rank_z").on(dve.memset(rank4[:, :, :, :], 0.0))
            need(dve, last_z)
            done = [last_z, last_z]
            for r in range(2):
                for t in range(T):
                    jk, sj = junk[:, t % 2, :], sjunk[:, t % 2, :]
                    need(dve, done[t % 2])
                    s = scol[:, r, t:t + 1]
                    k4 = rank4[:, r, t, :]
                    d = slice(t * P, (t + 1) * P)
                    if t > 0:
                        sig("rank").on(dve.tensor_scalar(jk[:, 0:t * P], srow[:, r, 0:t * P], s, 0.0, ALU.is_gt, ALU.add, accum_out=k4[:, 0:1]))
                    if t < T - 1:
                        sig("rank").on(dve.tensor_scalar(jk[:, (t + 1) * P:N], srow[:, r, (t + 1) * P:N], s, 0.0, ALU.is_ge, ALU.add, accum_out=k4[:, 1:2]))
                    yield
                    sig("rank").on(dve.scalar_tensor_tensor(out=sj[:, 0:P], in0=srow[:, r, d], scalar=s, in1=later[:, :],
                                                            op0=ALU.is_ge, op1=ALU.mult, accum_out=k4[:, 2:3]))
                    e = sig("rank").on(dve.scalar_tensor_tensor(out=sj[:, P:2 * P], in0=srow[:, r, d], scalar=s, in1=not_later[:, :],
                                                                op0=ALU.is_gt, op1=ALU.mult, accum_out=k4[:, 3:4]))
                    done[t % 2] = e
                    yield
                need(dve, e, done[0])
                e = sig("rank").on(dve.tensor_reduce(rank[:, r, :], rank4[:, r, :, :], AX_X, ALU.add))
                if r == 0:
                    rank_q = e
                yield
                while "proj_done" not in res:
                    yield
                need(dve, e, *([done[0], done[1]] if r else [res["proj_done"]]))
                for t in range(T):
                    res[f"onehot{r}"] = sig("onehot").on(dve.tensor_scalar(onehots[r][t], iota_row[:, :], rank[:, r, t:t + 1], None, ALU.is_equal))
                    if t % 2:
                        yield
            res["routed"] = e
            yield
            for h in range(2):
                need(pe, rank_q, free[MISC])
                for j in range(4):
                    ins = pe.transpose(bank[MISC][:, j * P:(j + 1) * P],
                                       rank[:, 0, 4 * h + j:4 * h + j + 1].broadcast_to([P, P]), ident[:, :])
                f = sig("srow_p").on(ins)
                need(act, f, res["routed"])
                free[MISC] = res["rank_row"] = sig("srow").on(act.activation(rank_row[:, h * 512:(h + 1) * 512], bank[MISC][:, :], ACT.Copy))
                yield

        def gather(res, rt):
            for r in range(2):
                b = TP + r
                need(pe, res[f"onehot{r}"], free[b], res["yr"])
                for c in range(C):
                    for t in range(T):
                        for part in range(2):
                            ins = pe.matmul(bank[b][:, c * NSEL:(c + 1) * NSEL], yr[part][:, t, c * P:(c + 1) * P], onehots[r][t],
                                            start=(t == 0 and part == 0), stop=(t == T - 1 and part == 1))
                oh_used = sig("gather").on(ins)
                need(act, oh_used, res["proj_done"])
                for c in range(C):
                    f = sig("hin").on(act.activation(hin[r][:, c, :], bank[b][:, c * NSEL:(c + 1) * NSEL], ACT.Copy, scale=gam_s[:, c:c + 1]))
                free[b] = f
                res[f"hin{r}"] = f
            res["x_free"] = oh_used
            n = 0
            for kind in ("q", "k"):
                w, r, dst = (wqh_s, 0, hq) if kind == "q" else (wkvh_s, 1, hk)
                for pr in range(2):
                    b = n % 4
                    need(pe, res[f"hin{r}"], free[b])
                    for j in range(2):
                        ch = 2 * pr + j
                        for c in range(C):
                            ins = pe.matmul(bank[b][:, j * NSEL:(j + 1) * NSEL], w[:, c, ch * P:(ch + 1) * P], hin[r][:, c, :],
                                            start=(c == 0), stop=(c == C - 1))
                    e = sig("hproj").on(ins)
                    need(act, e, res["proj_done"])
                    free[b] = res["hqkv"] = sig("hqkv").on(act.activation(
                        dst[:, 2 * pr:2 * pr + 2, :], bview(b, "p (j n) -> p j n", j=2), ACT.Copy,
                        scale=DH ** -0.5 if kind == "q" else 1.0))
                    n += 1
            for t in range(ST):
                b = n % 4
                need(pe, res["hin1"], free[b])
                for c in range(C):
                    ins = pe.matmul(bank[b][:, :], hin[1][:, c, t * P:(t + 1) * P], wkvh_s[:, c, INNER:2 * INNER],
                                    start=(c == 0), stop=(c == C - 1))
                e = sig("hproj").on(ins)
                need(act, e)
                free[b] = res["hqkv"] = sig("hqkv").on(act.activation(hv[:, t, :], bank[b][:, :], ACT.Copy))
                n += 1
            finish(rt)
            need(dve, res["rank_row"], oh_used)
            for kk in range(ST):
                res["rank_hot"] = sig("rank_hot").on(dve.tensor_scalar(rank_hot[:, kk, :], rank_row[:, :], iota_col[:, kk:kk + 1], None, ALU.is_equal))

        def attention(tiles, between, tile_done):
            items = [(n, hp) for n in range(len(tiles)) for hp in range(HEADS // 2)]
            soft, turned = {}, {}
            prob_free, probT_free = {}, {}
            o_ready, normed_of = {}, {}

            def head(hp, h):
                return hp // 2 * 4 + hp % 2 + 2 * h

            def scores(i):
                n, hp = items[i]
                tl = tiles[n]
                b = i % 2
                if hp == 0 and "before" in tl:
                    tl["before"]()
                need(pe, tl["ready"](), free[b])
                sv = bview(b, "p (h k) -> p h k", h=2)
                for h in range(2):
                    hs, ch = slice(hp % 2 * DH, (hp % 2 + 1) * DH), head(hp, h) // 2
                    ins = pe.matmul(sv[:, h, :], tl["q"](hs, ch), tl["k"](hs, ch),
                                    start=True, stop=True)
                e = sig("sim").on(ins)
                need(dve, e, soft.get(i - 4))
                pr = prob[i % NP]
                if tl["mask"] is None:
                    m = sig("nmax").on(dve.tensor_reduce(nmax[:, i % 4, :], sv, AX_X, ALU.max, negate=True))
                    src, sign = sv, 1.0
                else:
                    need(dve, prob_free.get(i - NP), last["ring"])
                    for h in range(2):
                        m = sig("nmax").on(dve.tensor_tensor_reduce(pr[:, h, :], sv[:, h, :], mask[:, tl["mask"], :], -1.0, 3e38,
                                                                    ALU.add, ALU.min, nmax[:, i % 4, h:h + 1]))
                    src, sign = pr, -1.0
                    free[b] = m
                need(act, m, prob_free.get(i - NP), last["ring"])
                if hp == 0:
                    need(act, normed_of.get(n - 2))
                for h in range(2):
                    e = sig("soft").on(act.activation(pr[:, h, :], src[:, h, :], ACT.Exp, bias=nmax[:, i % 4, h:h + 1], scale=sign,
                                                      accum_out=den[:, n % 2, head(hp, h):head(hp, h) + 1]))
                soft[i] = e
                if tl["mask"] is None:
                    free[b] = e

            def turn(i):
                b = 2 + i % 2
                need(pe, soft[i], free[b])
                for h in range(2):
                    for kk in range(2):
                        ins = pe.transpose(bank[b][:, (2 * h + kk) * P:(2 * h + kk + 1) * P],
                                           prob[i % NP][:, h, kk * P:(kk + 1) * P], ident[:, :])
                e = prob_free[i] = sig("probT_p").on(ins)
                src = bview(b, "p (a n) -> p a n", a=4)
                need(act, e, probT_free.get(i - 2), last["ring"])
                free[b] = turned[i] = sig("probT_a").on(act.activation(probT[i % 2][:, :, :], src, ACT.Copy))

            def values(i):
                n, hp = items[i]
                b = 4 + n % 2
                need(pe, turned[i])
                if hp == 0:
                    need(pe, free[b])
                for h in range(2):
                    hd = head(hp, h)
                    for kk in range(2):
                        ins = pe.matmul(bank[b][:, hd * DH:(hd + 1) * DH], probT[i % 2][:, 2 * h + kk, :], tiles[n]["v"](kk, hd),
                                        start=(kk == 0), stop=(kk == 1))
                e = probT_free[i] = sig("pv").on(ins)
                if hp == HEADS // 2 - 1:
                    need(dve, soft[i], last.get("rden"))
                    r = sig("rden").on(dve.reciprocal(rden[:, :], den[:, n % 2, :]))
                    need(dve, e, r, last.get("o_s"), last["ring"])
                    f = sig("o").on(dve.tensor_tensor(o_s[:, :].rearrange("p (h d) -> p h d", h=HEADS),
                                                      bview(b, "p (h d) -> p h d", h=HEADS),
                                                      rden[:, :].unsqueeze(2).broadcast_to([P, HEADS, DH]), ALU.mult))
                    last["rden"] = free[b] = o_ready[n] = normed_of[n] = f

            def out_turn(n):
                need(pe, o_ready[n], free[TP])
                for ch in range(HC):
                    ins = pe.transpose(bank[TP][:, ch * P:(ch + 1) * P], o_s[:, ch * P:(ch + 1) * P], ident[:, :])
                e = last["o_s"] = sig("oT_p").on(ins)
                need(act, e, last.get("oT_s"), last["ring"])
                f = free[TP] = sig("oT").on(act.activation(oT_s[:, :, :], bview(TP, "p (c n) -> p c n", c=HC), ACT.Copy))
                return f

            def out_proj(n, f):
                tl = tiles[n]
                if n == 0:
                    pe.wait_ge(late_loaded, late)
                need(pe, f, free[TP], *tl["extra_ready"]())
                ins = None
                for ch in range(HC):
                    ins = pe.matmul(bank[TP][:, 0:D], oT_s[:, ch, :], tl["wo"][:, ch, :], start=(ch == 0),
                                    stop=(ch == HC - 1 and not tl["extra"]))
                more = tl["extra"]
                for m, (lh, rh) in enumerate(more):
                    ins = pe.matmul(bank[TP][:, 0:D], lh, rh, start=False, stop=(m == len(more) - 1))
                e = last["oT_s"] = sig("y_out").on(ins)
                free[TP] = tl["sink"](bank[TP][:, 0:D], e)
                tile_done(n, free[TP])

            pend = []
            L = len(items)
            for s in range(L + 7):
                between(s)
                if 0 <= s - 2 < L:
                    turn(s - 2)
                if s < L:
                    scores(s)
                if 0 <= s - 3 < L:
                    values(s - 3)
                    if items[s - 3][1] == HEADS // 2 - 1:
                        pend.append((s, items[s - 3][0]))
                if pend and pend[0][0] + 1 == s:
                    oT_ev = out_turn(pend[0][1])
                if pend and pend[0][0] + 2 == s:
                    out_proj(pend.pop(0)[1], oT_ev)
            assert not pend
            return (sig("pv").sem, sig("pv").n)

        def row(b, peeled):
            res = [first, {}]
            prep = ffn_prep(1, xin, [], res[1])
            a0 = ffn_main(0, xin, x1, res[0], prep, "ffn1_0", stored_before=b * 16 + 16)
            ares = {}
            aprep = attn_prep(0, [a0], ares)
            until(prep, res[1], "xt")
            fill = chain(prep, aprep)
            a1 = ffn_main(1, xin, x1, res[1], fill, "ffn1_1", stored_before=b * 16 + 16)
            finish(fill)
            ares["x_free"] = ares["a1"] = a1
            last["ring"] = last[("h", (E - 1) % NH)]
            xl0 = dict(ares)
            aprep = attn_prep(1, [a1], ares)
            advance(aprep, PACE["attn"][0])
            rt = chain(aprep, routing(ares))
            for n, _ in enumerate(project_light(0, xl0, (0, 1, 2, 3))):
                advance(rt, PACE["project_0"][n])
            until(rt, ares, "scores_done")
            project = project_light(1, ares, (MISC, TP))
            advance(project, PACE["project_1"][-1])
            res2 = [{}, {}]
            summed, preps = {}, {}

            def scatter(t):
                return [(rank_hot[:, kk, t * P:(t + 1) * P], ho[part][:, kk, :]) for kk in range(ST) for part in range(2)]

            def light(t, fused):
                def sink(y, e):
                    need(dve, e)
                    summed[t] = sig("x2").on(dve.tensor_tensor(x1[:, t, :], y, x1[:, t, :], ALU.add))
                    return summed[t]
                return dict(
                    name=t, ready=lambda: (xl0 if t < TG - 1 else ares)["qkv"], mask=0 if t == 0 else 2 if t == T - 1 else 1, wo=wol_s, sink=sink,
                    extra=scatter(t) if fused else [],
                    extra_ready=lambda: [ares["ho"], ares["rank_hot"]] if fused else [],
                    q=lambda hs, ch: qT[hs, ch, t * P:(t + 1) * P],
                    k=lambda hs, ch: kT[hs, ch, t * P:t * P + KEYS],
                    v=lambda kk, hd: V[:, t + kk, hd * DH:(hd + 1) * DH])

            def start_heavy():
                until(rt, ares, "routed")
                pe.wait_ge(late_loaded, late)
                gather(ares, rt)
                if not peeled:
                    need(sp, ares["x_free"])
                    for g in range(G):
                        x_next[g] = sig(f"x_load{g}").on(sp.dma_start(xin[:, g * TG:(g + 1) * TG, :], x_next_src(b, g)), 16)

            def heavy(n):
                def sink(y, e):
                    need(act, e, ares["rank_hot"])
                    hi = sig("ho_hi").on(act.activation(ho[0][:, n, :], y, ACT.Copy))
                    need(dve, hi)
                    ares["ho"] = sig("ho_lo").on(dve.tensor_tensor(ho[1][:, n, :], y, ho[0][:, n, :].bitcast(F32), ALU.subtract))
                    return ares["ho"]
                tl = dict(
                    name=f"heavy{n}", ready=lambda: ares["hqkv"], mask=None, wo=woh_s, extra=[], extra_ready=lambda: [], sink=sink,
                    q=lambda hs, ch: hq[hs, ch, n * P:(n + 1) * P],
                    k=lambda hs, ch: hk[hs, ch, :],
                    v=lambda kk, hd: hv[:, kk, hd * DH:(hd + 1) * DH])
                if n == 0:
                    tl["before"] = start_heavy
                return tl

            EARLY = T - 4
            tiles = [light(t, False) for t in range(EARLY)] + [heavy(n) for n in range(ST)]
            tiles += [light(t, True) for t in range(EARLY, T)]

            def between(s):
                if s < (TG - 1) * HEADS // 2:
                    advance(project, PACE["project_1"][s])
                elif s == (TG - 1) * HEADS // 2:
                    finish(project)
                if s < EARLY * HEADS // 2:
                    advance(rt, PACE["routing"][s])
                elif 0 in preps:
                    advance(preps[0], PACE["ffn2_prep"][s - (T + ST - 4) * HEADS // 2])

            def tile_done(n, e):
                name = tiles[n]["name"]
                if name == f"heavy{ST - 1}":
                    last[("xt", 0)] = last[("xt", 1)] = e
                    for pr in range(EARLY // 2):
                        sbk = (MISC, TP)[pr % 2]
                        need(pe, ares["ho"], ares["rank_hot"], free[sbk])
                        for j in range(2):
                            parts = scatter(2 * pr + j)
                            for m, (lh, rh) in enumerate(parts):
                                ins = pe.matmul(bank[sbk][:, j * D:(j + 1) * D], lh, rh, start=(m == 0), stop=(m == len(parts) - 1))
                        e = sig("scatter").on(ins)
                        need(dve, e, summed[2 * pr + 1])
                        e = free[sbk] = sig("x2").on(dve.tensor_tensor(x1[:, 2 * pr:2 * pr + 2, :], bview(sbk, "p (t n) -> p t n", t=2),
                                                                        x1[:, 2 * pr:2 * pr + 2, :], ALU.add))
                    preps[0] = ffn_prep(0, x1, [e], res2[0])
                if name == T - 1:
                    until(preps[0], res2[0], "xt")
                    preps[1] = ffn_prep(1, x1, [e], res2[1])

            att = attention(tiles, between, tile_done)
            need(act, att)
            need(pool, att)
            f0 = ffn_main(0, x1, x1, res2[0], chain(preps[0], preps[1]), "ffn2_0")
            need(sp, f0)
            store(b, 0)
            nxt = {}
            until(preps[1], res2[1], "xt")
            prep = iter(()) if peeled else ffn_prep(0, xin, [x_next[0]], nxt)
            fill = chain(preps[1], prep)
            f1 = ffn_main(1, x1, x1, res2[1], fill, "ffn2_1")
            if not peeled:
                finish(fill)
            need(sp, f1)
            store(b, 1)
            if not peeled:
                need(dve, x_next[1])

        x_next = {}

        def x_next_src(b, g):
            return x_v[bass.ds(b + 1, 1), :, g * TG:(g + 1) * TG, :].rearrange("b p t d -> p (b t) d")

        def store(b, g):
            gs = slice(g * TG, (g + 1) * TG)
            if isinstance(b, int):
                dst = out_v[b, :, gs, :]
            else:
                dst = out_v[bass.ds(b, 1), :, gs, :].rearrange("b p t d -> p (b t) d")
            sp.dma_start(dst, x1[:, gs, :]).then_inc(stored[g], 16)

        def new_counts():
            nc.all_engine_barrier()
            pool.sem_clear(clear_range())
            nc.all_engine_barrier()
            for s in sems.values():
                s.n = 0
            waited.clear()
            last.clear()
            for i in range(8):
                free[i] = None

        def clear_range():
            nums = sorted(s.sem.num for s in sems.values())
            assert nums == list(range(nums[0], nums[-1] + 1)), nums
            return range(nums[0], nums[-1] + 1)

        for e_ in (pe, act, dve, pool):
            need(e_, consts)
        first = {}
        prep, splits = ffn_prep(0, xin, [x_ready[0]], first), split_weights()
        for n_, m_ in PACE["start"]:
            advance(prep, n_)
            if m_ == 1:
                need(dve, bias_loaded)
            advance(splits, m_)
        finish(prep)
        finish(splits)
        need(pool, res_w["split"])
        for side in (slice(0, HALO), slice(HALO + N, PADDED)):
            k.on(pool.memset(kT[:, :, side], 0.0))
        need(act, bias_loaded)
        need(dve, x_ready[1])
        names = ("gT_hi xl_f xl_lo norm norm_a score yr_hi yr_lo hidden gelu h_lo expert acc bias2 proj q srow_p srow rank_z rank "
                 "onehot gather hin rank_hot hproj hqkv sim nmax soft probT_p probT_a pv rden o oT_p oT y_out ho_hi ho_lo x2 scatter").split()
        for n_ in names:
            sig(n_)
        new_counts()
        first = dict.fromkeys(("xt", "gate", "gT"))
        with nc.Fori(0, ROWS - 1) as b:
            row(b, False)
            new_counts()
        row(ROWS - 1, True)
        for s_ in stored:
            sp.wait_ge(s_, 16 * ROWS + 16)
        nc.all_engine_barrier()


_INS = ["L0_attn_x", "L0_attn_gamma_h", "L0_attn_wq_h", "L0_attn_wkv_h", "L0_attn_wo_h", "L0_attn_ln_g", "L0_attn_ln_b",
        "L0_attn_wqkv_l", "L0_attn_wo_l", "L0_attn_rt_q", "L0_attn_rt_kv", "L0_ffn_router_w", "L0_ffn_router_b",
        "L0_ffn_W1", "L0_ffn_b1", "L0_ffn_W2", "L0_ffn_b2"]


def kernel(**inputs):
    import concourse.bacc as bacc
    from concourse.bass_utils import run_bass_kernel_spmd

    nc = bacc.Bacc("TRN2", target_bir_lowering=False, num_devices=1)
    arrays, args = {}, []
    for name in _INS:
        a = np.ascontiguousarray(inputs[name])
        arrays[f"in_{name}"] = a
        args.append(nc.dram_tensor(f"in_{name}", a.shape, mybir.dt.from_np(a.dtype), kind="ExternalInput").ap())
    shape = arrays["in_L0_attn_x"].shape
    args.append(nc.dram_tensor("out_0", shape, F32, kind="ExternalOutput").ap())
    build(nc, *args)
    r = run_bass_kernel_spmd(nc, [arrays], core_ids=[0])
    return r.results[0]["out_0"]
```

```python
from contextlib import ExitStack
from itertools import chain

import numpy as np

import concourse.bass as bass
from concourse import mybir

F32 = mybir.dt.float32
F32R = mybir.dt.float32r
BF16 = mybir.dt.bfloat16
I32 = mybir.dt.int32
ALU = mybir.AluOpType
ACT = mybir.ActivationFunctionType
AX_X = mybir.AxisListType.X

P = 128
WIN = 64
KEYS = 4 * WIN
HALO = WIN
NSEL = 256
HEADS, DH = 8, 64
LN_EPS = 1e-5
NORM_MIN = 1e-12
MASKED = -1e30

PACE = dict(
    ffn1_0=(0, 1, 1, 2, 0, 0, 0, 1, 0, 2),
    ffn1_1=(1, 0, 1, 1, 0, 1, 1, 2, 2, 1),
    ffn2_0=(1, 1, 1, 1, 1, 2, 1, 1, 1, 0),
    ffn2_1=(1, 1, 0, 1, 1, 1, 3, 0, 0, 2),
    project_0=(2, 0, 2, 1, 2, 0, 2, 1, 4, 1, 1, 0),
    project_1=(1, 1, 1, 1, 1, 1, 1, 1, 1, 1, 1, 1, 1),
    attn=(2,),
    routing=(3, 3, 3, 3, 3, 3, 3, 3, 3, 3, 3, 3, 4, 2, 3, 3, 3, 3, 3, 3, 3, 3, 3, 3),
    ffn2_prep=(1, 0, 1, 0, 1, 1, 1, 0, 1, 1, 0, 1, 1, 1, 1, 1, 1, 2, 1, 1, 1, 1, 1, 1),
    bias=(6, 7),
    start=((1, 1), (1, 0), (1, 0), (1, 1), (1, 1), (1, 1), (1, 1)),
    via_ffn1_0=(3, 7),
    via_ffn1_1=(),
    via_ffn2_0=(2, 4, 6, 7),
    via_ffn2_1=(1, 6),
)


class Signal:

    def __init__(self, sem):
        self.sem, self.n = sem, 0

    def on(self, ins, by=1):
        ins.then_inc(self.sem, by)
        self.n += by
        return self.sem, self.n


def build(nc, x_in, gamma_h, wq_h, wkv_h, wo_h, ln_g, ln_b, wqkv, wo_l, rt_q, rt_kv,
          router_w, router_b, w1, b1, w2, b2, out):
    pe, act, dve, pool, sp = nc.tensor, nc.scalar, nc.vector, nc.gpsimd, nc.sync
    ROWS, N, D = x_in.shape
    E, _, FF = w1.shape
    T = N // P
    C = D // P
    INNER = HEADS * DH
    HC = INNER // P
    G = 2
    TG = T // G
    NG = TG * P
    ST = NSEL // P
    PADDED = N + 2 * HALO
    BIAS_AT = tuple(PACE["bias"])
    assert FF == P and KEYS == NSEL and HC == 4 and TG == 4

    ctx = ExitStack()
    with ctx:
        sems = {}

        def sig(name):
            if name not in sems:
                sems[name] = Signal(ctx.enter_context(nc.semaphore(name)))
            return sems[name]

        def need(eng, *events):
            for e in events:
                if e is None:
                    continue
                if isinstance(e, list):
                    need(eng, *e)
                    continue
                key = (str(eng.engine), str(e[0]))
                if waited.get(key, 0) < e[1]:
                    waited[key] = e[1]
                    eng.wait_ge(*e)

        waited = {}

        top = [-(-nc.sbuf_base // 64) * 64]

        def place(nbytes):
            at = top[0]
            top[0] += -(-nbytes // 64) * 64
            assert top[0] <= nc.sbuf_usable_end, top[0]
            return at

        def at(name, shape, dt, offset):
            return nc.alloc_sbuf_tensor_at(name, shape, dt, offset=offset)

        def sb(name, shape, dt=F32):
            size = int(np.prod(shape[1:])) * (2 if dt == BF16 else 4)
            return at(name, shape, dt, place(size))

        def pair(name, shape):
            return sb(name + "_hi", shape, F32R), sb(name + "_lo", shape, F32R)

        w1_s = pair("w1", [P, C, E, FF])
        w2_s = pair("w2", [P, E, D])
        wqkv_s = pair("wqkv", [P, C, 3 * INNER])
        rw_s = sb("rw", [P, C, 2, E], F32R)
        wqh_s = sb("wqh", [P, C, INNER])
        wkvh_s = sb("wkvh", [P, C, 2 * INNER])
        wol_s = sb("wol", [P, HC, D])
        woh_s = sb("woh", [P, HC, D])
        b2_s = sb("b2s", [64 + E, D], F32R)
        b1_s = sb("b1s", [P, E])
        rb_s = sb("rbs", [P, E])
        gam_s = sb("gams", [P, C])
        lng_s = sb("lngs", [P, C])
        lnb_s = sb("lnbs", [P, C])
        rt_s = sb("rts", [P, 2, D])
        ident = sb("ident", [P, P])
        iota_row = sb("iota_row", [P, NSEL])
        iota_col = sb("iota_col", [P, ST])
        later = sb("later", [P, P], BF16)
        not_later = sb("not_later", [P, P], BF16)
        lower_e = sb("lower_e", [P, E, E], BF16)
        minus_half = sb("minus_half", [P, TG])
        euler = sb("euler", [P, TG])
        gT = sb("gT", [64 + E, TG, P], F32R)
        mask = sb("mask", [P, 3, KEYS], BF16)

        x_off = place(N * D // P * 4)
        xin = at("xin", [P, T, D], F32, x_off)
        srow = at("srow", [P, 2, N], F32, x_off)
        onehot_kv = at("onehot_kv", [P, T, NSEL], F32R, x_off)
        x1 = sb("x1", [P, T, D])
        yr_off = place(2 * T * D * 4)
        yr = (at("yr_hi", [P, T, D], F32R, yr_off), at("yr_lo", [P, T, D], F32R, yr_off + T * D * 4))
        rank_hot = at("rank_hot", [P, ST, N], F32R, yr_off)
        ho = (at("ho_hi", [P, ST, D], F32R, yr_off + ST * N * 4),
              at("ho_lo", [P, ST, D], F32R, yr_off + ST * N * 4 + ST * D * 4))
        xt_off = place(2 * C * PADDED * 4)
        xt = (at("xt_hi", [P, C, PADDED], F32R, xt_off),
              at("xt_lo", [P, C, PADDED], F32R, xt_off + C * PADDED * 4))
        q_off = top[0]
        qT = sb("qT", [P, HC, N])
        kT = sb("kT", [P, HC, PADDED])
        V = sb("V", [P, T + 1, INNER])
        v_tile = lambda name, t: at(name, [P, TG, D], F32, q_off + (HC * N + HC * PADDED + t * INNER) * 4)
        z_of = [v_tile("z0", TG + 1), v_tile("z1", TG + 3)]
        gated = at("gated", [P, 2, D], F32, q_off)
        y1_t = v_tile("y1", TG + 1)
        half = HALO * 4
        onehot_q = [at(f"onehot_q{n}", [P, T // 2, NSEL], F32R, xt_off + half + n * PADDED * 4) for n in range(2)]
        onehots = [[onehot_q[t // (T // 2)][:, t % (T // 2), :] for t in range(T)], [onehot_kv[:, t, :] for t in range(T)]]
        hin = [at(f"hin{r}", [P, C, NSEL], F32, xt_off + half + r * C * NSEL * 4) for r in range(2)]
        hq = at("hq", [P, HC, NSEL], F32, xt_off + half + PADDED * 4)
        hk = at("hk", [P, HC, NSEL], F32, xt_off + half + 2 * PADDED * 4)
        hv = at("hv", [P, ST, INNER], F32, xt_off + half + 3 * PADDED * 4)
        NP = 3
        ring = place((NP * 2 * KEYS + 2 * 4 * P + 2 * INNER) * 4)
        NH = 3
        hf = [at(f"hf{i}", [P, NG], F32, ring + i * NG * 4) for i in range(NH)]
        hl = [at(f"hl{i}", [P, NG], F32R, ring + i * NG * 4) for i in range(NH)]
        hh = [at(f"hh{i}", [P, NG], F32R, ring + (NH + i) * NG * 4) for i in range(NH)]
        prob = [at(f"prob{i}", [P, 2, KEYS], F32, ring + i * 2 * KEYS * 4) for i in range(NP)]
        probT = [at(f"probT{i}", [P, 4, P], F32, ring + (NP * 2 * KEYS + i * 4 * P) * 4) for i in range(2)]
        o_s = at("o_s", [P, INNER], F32, ring + (NP * 2 * KEYS + 8 * P) * 4)
        oT_s = at("oT_s", [P, HC, P], F32, ring + (NP * 2 * KEYS + 8 * P + INNER) * 4)
        y_off = place(TG * D * 4)
        y_t = at("y_t", [P, TG, D], F32, y_off)
        y_of = [y_t, y1_t]
        junk = at("junk", [P, 2, N], mybir.dt.uint8, y_off)
        sjunk = at("sjunk", [P, 2, D], mybir.dt.uint8, y_off + 2 * N)
        rank_row = at("rank_row", [P, N], F32, y_off)
        cmp_g = at("cmp_g", [P, TG, E, E], BF16, y_off)
        cmp_e = at("cmp_e", [P, TG, E, E], BF16, y_off + TG * E * E * 2)
        xf_t = at("xf_t", [P, C, 2 * P], F32, ring + 6 * NG * 4)
        st = sb("st", [P, TG, 6])
        mv = sb("mv", [P, TG, 2])
        vt = sb("vt", [P, TG])
        rs = sb("rs", [P, TG])
        rn = sb("rn", [P, G, TG])
        nm = sb("nm", [P, TG])
        scol = sb("scol", [P, 2, T])
        rank4 = sb("rank4", [P, 2, T, 4])
        rank = sb("rank", [P, 2, T])
        lg = sb("lg", [P, TG, E])
        lmax = sb("lmax", [P, TG])
        lrank = sb("lrank", [P, TG, E])
        l2nd = sb("l2nd", [P, TG, E])
        wt = sb("wt", [P, 2, TG])
        place_1 = sb("place_1", [P, TG, E])
        t2nd = sb("t2nd", [P, TG])
        gate = sb("gate", [P, G, TG, E])
        nmax = sb("nmax", [P, 4, 2])
        den = sb("den", [P, 2, HEADS])
        rden = sb("rden", [P, HEADS])

        bank = [ctx.enter_context(nc.psum_tensor(f"bank{i}", [P, 512], F32)) for i in range(8)]
        free = [None] * 8
        TP, MISC = 6, 7

        def bview(i, pattern, **kw):
            return bank[i][:, :].rearrange(pattern, **kw)

        def mm3(o, w, x, start=True, stop=True):
            pe.matmul(o, w[0], x[0], start=start, stop=False)
            pe.matmul(o, w[1], x[0], start=False, stop=False)
            return pe.matmul(o, w[0], x[1], start=False, stop=stop)

        def bcast_rows(v, n):
            return v.rearrange("(a n) -> a n", a=1).broadcast_to([P, n])

        b2_f = at("b2_f", [E, D], F32, ring + 4096)
        wst = at("wst", [P, 2 * P * C * E + C * 3 * INNER + C * E], F32, q_off)
        loads = [
            (lambda o: o.rearrange("p (c n) -> p c n", c=C), router_w.rearrange("(c p) n -> p c n", p=P), [rw_s[:, :, n, :] for n in range(2)], C * E),
            (lambda o: o.rearrange("p (c e f) -> p c e f", c=C, e=E), w1.rearrange("e (c p) f -> p c e f", p=P), w1_s, C * E * FF),
            (lambda o: o.rearrange("p (e n) -> p e n", e=E), w2.rearrange("e p n -> p e n"), w2_s, E * D),
            (lambda o: o.rearrange("p (c n) -> p c n", c=C), wqkv.rearrange("(c p) n -> p c n", p=P), wqkv_s, C * 3 * INNER),
        ]
        late_loaded = ctx.enter_context(nc.semaphore("late_loaded"))
        stored = [ctx.enter_context(nc.semaphore(f"stored{g}")) for g in range(G)]
        for s_ in stored:
            sp.sem_inc(s_, 16)
        x_v = x_in.rearrange("b (t p) d -> b p t d", p=P)
        out_v = out.rearrange("b (t p) d -> b p t d", p=P)

        x_ready = {}

        def load_first(g):
            x_ready[g] = sig(f"x_load{g}").on(sp.dma_start(xin[:, g * TG:(g + 1) * TG, :], x_v[0, :, g * TG:(g + 1) * TG, :]), 16)

        load_first(0)
        o = 0
        views = []
        for shape, src, dst, n in loads:
            v = shape(wst[:, o:o + n])
            for c in range(src.shape[1]):
                ev = sig(f"w_load{len(views)}").on(sp.dma_start(v[:, c], src[:, c]), 16)
            views.append((wst[:, o:o + n], dst, ev))
            o += n
            if dst is w1_s:
                load_first(1)
        for dst, src in ((rb_s[:, :], bcast_rows(router_b, E)), (b1_s[:, :], b1.rearrange("e f -> f e"))):
            bias_loaded = sig("bias_load").on(act.dma_start(dst, src, allow_slow_non_contiguous=True), 16)
        for dst, src in ((b2_f[:, :], b2), (gam_s[:, :], gamma_h.rearrange("(c p) -> p c", p=P)),
                         (lng_s[:, :], ln_g.rearrange("(c p) -> p c", p=P)), (lnb_s[:, :], ln_b.rearrange("(c p) -> p c", p=P)),
                         (rt_s[:, 0, :], bcast_rows(rt_q, D)), (rt_s[:, 1, :], bcast_rows(rt_kv, D))):
            small = sig("c_load").on(sp.dma_start(dst, src, allow_slow_non_contiguous=True), 16)
        late = 0
        for dst, src in ((wqh_s[:, :, :], wq_h.rearrange("(c p) n -> p c n", p=P)),
                         (wkvh_s[:, :, :], wkv_h.rearrange("(c p) n -> p c n", p=P)),
                         (wol_s[:, :, :], wo_l.rearrange("(c p) n -> p c n", p=P)),
                         (woh_s[:, :, :], wo_h.rearrange("(c p) n -> p c n", p=P))):
            sp.dma_start(dst, src).then_inc(late_loaded, 16)
            late += 16

        def flat(t):
            if t.shape[-1] == E:
                return t
            return t[:].rearrange({3: "p a b -> p (a b)", 4: "p a b c -> p (a b c)"}[len(t.shape)])

        def split_weights():
            for src, dst, ev in views:
                if dst[0].shape[-1] == E:
                    src = src.rearrange("p (c n) -> p c n", c=C)
                need(act, ev)
                hi = sig("w_hi").on(act.activation(flat(dst[0]), src, ACT.Copy))
                need(dve, ev, hi)
                res_w["split"] = sig("w_lo").on(dve.tensor_tensor(flat(dst[1]), src, flat(dst[0]).bitcast(F32), ALU.subtract))
                yield
            need(act, small, b2_zero)
            for at_ in (0, 32):
                hi = sig("w_hi").on(act.activation(b2_s[at_:at_ + E, :], b2_f[:, :], ACT.Copy))
            need(dve, hi)
            sig("w_lo").on(dve.tensor_tensor(b2_s[64:64 + E, :], b2_f[:, :], b2_s[0:E, :].bitcast(F32), ALU.subtract))
            yield

        res_w = {}

        k = sig("const")
        need(pool, k.on(pool.memset(gT[:].bitcast(F32), 0.0)))
        b2_zero = k.on(pool.memset(b2_s[:].bitcast(F32), 0.0))
        need(pool, b2_zero)
        k.on(pool.memset(ident[:], 0.0))
        k.on(pool.memset(later[:], 0.0))
        k.on(pool.memset(not_later[:], 1.0))
        k.on(pool.memset(lower_e[:], 1.0))
        k.on(pool.memset(minus_half[:], -0.5))
        k.on(pool.memset(euler[:], float(np.e)))
        k.on(pool.memset(mask[:], 0.0))
        for part in xt:
            for side in (slice(0, HALO), slice(HALO + N, PADDED)):
                k.on(pool.memset(part[:, :, side].bitcast(F32), 0.0))
        iota_i = at("iota_i", [P, NSEL + ST], I32, ring)
        c0 = k.on(pool.iota(iota_i[:, 0:NSEL], pattern=[[1, NSEL]], base=0, channel_multiplier=0))
        c0 = k.on(pool.iota(iota_i[:, NSEL:NSEL + ST], pattern=[[P, ST]], base=0, channel_multiplier=1))
        need(pool, c0)
        k.on(pool.tensor_copy(iota_row[:, :], iota_i[:, 0:NSEL]))
        k.on(pool.tensor_copy(iota_col[:, :], iota_i[:, NSEL:NSEL + ST]))
        k.on(pool.affine_select(out=ident[:, :], in_=ident[:, :], compare_op=ALU.not_equal, fill=1.0,
                                base=0, pattern=[[-1, P]], channel_multiplier=1))
        k.on(pool.affine_select(out=later[:, :], in_=later[:, :], compare_op=ALU.is_ge, fill=1.0,
                                base=0, pattern=[[-1, P]], channel_multiplier=1))
        k.on(pool.affine_select(out=not_later[:, :], in_=not_later[:, :], compare_op=ALU.is_ge, fill=0.0,
                                base=0, pattern=[[-1, P]], channel_multiplier=1))
        c0 = k.on(pool.affine_select(out=lower_e[:, :, :], in_=lower_e[:, :, :], compare_op=ALU.is_ge, fill=0.0,
                                base=-1, pattern=[[1, E], [-1, E]], channel_multiplier=0))
        need(pool, c0)
        for w in range(2):
            rows_w = slice(w * WIN, (w + 1) * WIN)
            dead = slice(3 * WIN, KEYS) if w == 0 else slice(0, WIN)
            k.on(pool.memset(mask[rows_w, :, dead], MASKED))
        k.on(pool.memset(mask[WIN:P, 2, 3 * WIN:KEYS], MASKED))
        consts = k.on(pool.memset(mask[0:WIN, 0, 0:WIN], MASKED))

        def ln_stats(srcs, after, key):
            need(dve, *after)
            for j, s in enumerate(srcs):
                e = sig("bn").on(dve.bn_stats(st[:, j, :], s))
            need(dve, e)
            for j in range(len(srcs)):
                e = sig("bn_aggr").on(dve.bn_aggr(mv[:, j, :], st[:, j, :]))
            need(pool, e)
            e = sig("var_eps").on(pool.tensor_scalar(vt[:, :], mv[:, :, 1], LN_EPS, None, ALU.add))
            m = sig("var_eps").on(pool.tensor_scalar(nm[:, :], mv[:, :, 0], -1.0, None, ALU.mult))
            need(pool, e)
            e = sig("rstd").on(pool.tensor_tensor(rs[:, :], vt[:, :], minus_half[:, :], ALU.pow))
            need(pool, e, m)
            return sig("rstd").on(pool.tensor_tensor(nm[:, :], nm[:, :], rs[:, :], ALU.mult))

        def normalise(dst, src, q):
            return sig("norm_a").on(act.activation(dst, src, ACT.Identity, bias=nm[:, q:q + 1], scale=rs[:, q:q + 1]))

        last = {}
        in_use = {"gT": False, "TP": False}

        def transposed(g, pr, kind, srcs, ready):
            tb = MISC if in_use["TP"] else (TP, MISC)[pr]
            need(pe, ready, free[tb])
            tp = bview(tb, "p (c n) -> p c n", c=C)
            for j in range(2):
                for c in range(C):
                    ins = pe.transpose(tp[:, c, j * P:(j + 1) * P], srcs[j][:, c * P:(c + 1) * P], ident[:, :])
            e = sig("xpose").on(ins)
            last["y_t" if kind == "ffn" else "z_turned"] = e
            col = HALO + (g * TG + pr * 2) * P
            hi, lo = (part[:, :, col:col + 2 * P] for part in xt)
            need(act, e, last.get(("xt", g)), last.get("xf"))
            if kind == "ffn":
                e1 = sig("xt_hi").on(act.activation(hi, tp, ACT.Copy))
                need(dve, e1, last.get(("xt", g)))
                e2 = sig("xt_lo").on(dve.tensor_tensor(lo, tp, hi.bitcast(F32), ALU.subtract))
                free[tb] = e2
                return e2
            for c in range(C):
                for dst in (hi, xf_t):
                    e1 = sig("xl_f").on(act.activation(dst[:, c, :], tp[:, c, :], ACT.Identity,
                                                       bias=lnb_s[:, c:c + 1], scale=lng_s[:, c:c + 1]))
            free[tb] = e1
            need(pool, e1, last.get(("xt", g)))
            e2 = sig("xl_lo").on(pool.tensor_tensor(lo, xf_t[:, :, :], hi.bitcast(F32), ALU.subtract))
            last["xf"] = e2
            return e2

        def ffn_prep(g, src, after, res):
            tiles = [src[:, g * TG + j, :] for j in range(TG)]
            rstd = ln_stats(tiles, after, "ffn")
            yield
            need(act, rstd, last.get("y_t"))
            e = {}
            for q in range(TG):
                e[q // 2] = normalise(y_t[:, q, :], tiles[q], q)
                if q % 2:
                    yield
            for pr in range(2):
                xt_ready = transposed(g, pr, "ffn", [y_t[:, 2 * pr + j, :] for j in range(2)], e[pr])
                if pr == 0:
                    yield
            res["xt"] = xt_ready
            yield

        def ffn_route(g, res):
            tb = MISC if in_use["TP"] else TP
            need(pe, res["xt"], free[tb])
            lgp = bank[tb][:, 0:TG * 2 * E].rearrange("p (t w e) -> p t w e", w=2, e=E)
            for j in range(TG):
                col = HALO + (g * TG + j) * P
                for c in range(C):
                    for n, part in enumerate(xt):
                        ins = pe.matmul(lgp[:, j, :, :], part[:, c, col:col + P], rw_s[:, c, :, :],
                                        start=(c == 0 and n == 0), stop=(c == C - 1 and n == 1))
            e = sig("logits").on(ins)
            need(dve, e, last.get("lg"))
            e = sig("lg").on(dve.tensor_tensor(lg[:, :, :], lgp[:, :, 0, :], rb_s[:, :].unsqueeze(1).broadcast_to([P, TG, E]), ALU.add))
            need(dve, e)
            e = free[tb] = sig("lg").on(dve.tensor_tensor(lg[:, :, :], lgp[:, :, 1, :], lg[:, :, :], ALU.add))
            yield
            need(dve, e)
            sig("lmax").on(dve.tensor_reduce(lmax[:, :], lg[:, :, :], AX_X, ALU.max))
            by_j = lg[:, :, :].unsqueeze(2).broadcast_to([P, TG, E, E])
            by_e = lg[:, :, :].unsqueeze(3).broadcast_to([P, TG, E, E])
            sig("cmp").on(dve.tensor_tensor(cmp_g[:, :, :, :], by_j, by_e, ALU.is_gt))
            e = sig("cmp").on(dve.tensor_tensor(cmp_e[:, :, :, :], by_j, by_e, ALU.is_equal))
            need(dve, e)
            e = sig("cmp").on(dve.tensor_tensor(cmp_e[:, :, :, :], cmp_e[:, :, :, :],
                                                lower_e[:, :, :].unsqueeze(1).broadcast_to([P, TG, E, E]), ALU.mult))
            need(dve, e, (sig("lmax").sem, sig("lmax").n))
            e = sig("cmp").on(dve.tensor_tensor(cmp_g[:, :, :, :], cmp_g[:, :, :, :], cmp_e[:, :, :, :], ALU.add))
            need(dve, e)
            last["lg"] = last["y_t"] = e = sig("cmp").on(dve.tensor_reduce(lrank[:, :, :], cmp_g[:, :, :, :], AX_X, ALU.add))
            yield
            need(dve, e)
            e = last["lg"] = sig("cmp").on(dve.scalar_tensor_tensor(out=l2nd[:, :, :], in0=lrank[:, :, :], scalar=1.0,
                                                                    in1=lg[:, :, :], op0=ALU.is_equal, op1=ALU.mult))
            need(dve, e)
            e = sig("cmp").on(dve.tensor_reduce(t2nd[:, :], l2nd[:, :, :], AX_X, ALU.add))
            need(dve, e)
            e = sig("cmp").on(dve.tensor_tensor(t2nd[:, :], t2nd[:, :], lmax[:, :], ALU.subtract))
            need(pool, e)
            e = sig("exp").on(pool.tensor_tensor(t2nd[:, :], euler[:, :], t2nd[:, :], ALU.pow))
            yield
            need(dve, e)
            e = sig("cmp").on(dve.tensor_scalar(wt[:, 0, :], t2nd[:, :], 1.0, 2.0, ALU.add, ALU.mult))
            need(dve, e)
            e = sig("cmp").on(dve.reciprocal(wt[:, 0, :], wt[:, 0, :]))
            need(dve, e)
            e = sig("cmp").on(dve.tensor_tensor(wt[:, 1, :], t2nd[:, :], wt[:, 0, :], ALU.mult))
            need(dve, e)
            w_of = [wt[:, n, :].unsqueeze(2).broadcast_to([P, TG, E]) for n in range(2)]
            need(dve, last.get(("gate", g)))
            sig("cmp").on(dve.scalar_tensor_tensor(out=place_1[:, :, :], in0=lrank[:, :, :], scalar=1.0, in1=w_of[1],
                                                   op0=ALU.is_equal, op1=ALU.mult))
            e = sig("cmp").on(dve.scalar_tensor_tensor(out=gate[:, g, :, :], in0=lrank[:, :, :], scalar=0.0, in1=w_of[0],
                                                       op0=ALU.is_equal, op1=ALU.mult))
            need(dve, e)
            gate_ready = sig("gate").on(dve.tensor_tensor(gate[:, g, :, :], gate[:, g, :, :], place_1[:, :, :], ALU.add))
            res["gate"] = gate_ready
            yield

        def gates_turned(g, res):
            while in_use["gT"]:
                yield
            in_use["gT"] = True
            need(pe, res["gate"], free[MISC])
            for j in range(TG):
                ins = pe.transpose(bank[MISC][0:E, j * P:(j + 1) * P], gate[:, g, j, :], ident[:, :])
            e = sig("gateT").on(ins)
            need(act, e, last.get("gT"))
            gp = bview(MISC, "p (t n) -> p t n", t=TG)[0:E]
            for at_ in (0, 64):
                e = sig("gT_hi").on(act.activation(gT[at_:at_ + E, :, :], gp, ACT.Copy))
            need(dve, e, last.get("gT"))
            free[MISC] = res["gT"] = sig("gT").on(dve.tensor_tensor(gT[32:32 + E, :, :], gp, gT[0:E, :, :].bitcast(F32), ALU.subtract))

        def route_and_turn(g, res):
            return chain(ffn_route(g, res), gates_turned(g, res))

        def advance(gen, n=1):
            for _ in range(n):
                if gen is not None and next(gen, "end") == "end":
                    return

        def until(gen, res, key):
            while key not in res:
                advance(gen)

        def finish(gen):
            for _ in gen:
                pass

        def ffn_main(g, src, dst, res, fill, pace, stored_before=None):
            cols = HALO + g * NG
            hid = {}
            acc = {}
            assert 0 not in PACE["via_" + pace]
            for s_ in range(E + 2):
                if s_ < E:
                    b, r = s_ % 2, s_ % NH
                    need(pe, res["xt"], free[b])
                    for c in range(C):
                        ins = mm3(bank[b][:, :], [w[:, c, s_, :] for w in w1_s], [w[:, c, cols:cols + NG] for w in xt],
                                  start=(c == 0), stop=(c == C - 1))
                    h = sig("hidden").on(ins)
                    last[("xt", g)] = h
                    need(act, h, last.get(("h", r)))
                    for dst_h in (hf[r], hh[r]):
                        f = free[b] = sig("gelu").on(act.activation(dst_h[:, :], bank[b][:, :], ACT.Gelu, bias=b1_s[:, s_:s_ + 1]))
                    need(pool, f)
                    hid[s_] = sig("h_lo").on(pool.tensor_tensor(hl[r][:, :], hf[r][:, :], hh[r][:, :].bitcast(F32), ALU.subtract))
                if s_ >= 2:
                    q = s_ - 2
                    until(fill, res, "gate")
                    if q == 0 and stored_before is not None:
                        dve.wait_ge(stored[g], stored_before)
                    b, r = q % 2, q % NH
                    need(pe, hid[q])
                    for pr in range(2):
                        ob = 2 + 2 * b + pr
                        need(pe, free[ob])
                        for j in range(2):
                            cs = slice((2 * pr + j) * P, (2 * pr + j + 1) * P)
                            ins = mm3(bank[ob][:, j * D:(j + 1) * D], [hh[r][:, cs], hl[r][:, cs]], [w[:, q, :] for w in w2_s])
                        oe = sig("expert").on(ins)
                        last[("h", r)] = oe
                        if pr == 0 or q not in PACE["via_" + pace]:
                            for j in range(2):
                                t = 2 * pr + j
                                need(dve, oe, res["gate"], acc.get(t))
                                xt_, at_ = dst[:, g * TG + t, :], src[:, g * TG + t, :]
                                acc[t] = sig("acc").on(dve.scalar_tensor_tensor(
                                    out=xt_, in0=bank[ob][:, j * D:(j + 1) * D], scalar=gate[:, g, t, q:q + 1],
                                    in1=at_ if q == 0 else xt_,
                                    op0=ALU.mult, op1=ALU.add))
                            free[ob] = acc[t]
                        else:
                            need(act, oe, res["gate"], acc.get("gated"))
                            for j in range(2):
                                free[ob] = acc["gate_read"] = sig("gated").on(act.activation(
                                    gated[:, j, :], bank[ob][:, j * D:(j + 1) * D], ACT.Copy, scale=gate[:, g, 2 + j, q:q + 1]))
                            need(pool, free[ob], acc[2], acc[3])
                            here = dst[:, g * TG + 2:g * TG + 4, :]
                            acc["gated"] = acc[2] = acc[3] = sig("acc_p").on(pool.tensor_tensor(here, gated[:, :, :], here, ALU.add))
                if s_ in BIAS_AT:
                    until(fill, res, "gT")
                    pr = BIAS_AT.index(s_)
                    need(pe, res["gT"], free[MISC])
                    for j in range(2):
                        ins = pe.matmul(bank[MISC][:, j * D:(j + 1) * D], gT[:, 2 * pr + j, :], b2_s[:, :], start=True, stop=True)
                    e = last["gT"] = sig("bias2").on(ins)
                    in_use["gT"] = pr == 0
                    need(dve, e, acc[2 * pr], acc[2 * pr + 1])
                    here = dst[:, g * TG + 2 * pr:g * TG + 2 * pr + 2, :]
                    acc[2 * pr] = acc[2 * pr + 1] = free[MISC] = sig("acc").on(dve.tensor_tensor(
                        here, bview(MISC, "p (t n) -> p t n", t=2), here, ALU.add))
                advance(fill, PACE[pace][s_])
            done = [acc[1], acc[2], acc[3]]
            last["gated"] = acc.get("gated")
            last[("gate", g)] = [acc[1], acc[3], acc.get("gate_read")]
            return done

        def light_prep(g, after, res):
            tiles = [x1[:, g * TG + j, :] for j in range(TG)]
            ys, zs = [y_of[g][:, j, :] for j in range(TG)], [z_of[g][:, j, :] for j in range(TG)]
            rstd = ln_stats(tiles, after, "attn")
            yield
            need(act, rstd, *after, last.get("z_turned") if g else last.get("y_t"))
            for j in range(TG):
                y = normalise(ys[j], tiles[j], j)
            yield
            rstd = ln_stats(ys, [y], "z")
            n = rn[:, g, :]
            e = sig("norm").on(pool.tensor_tensor(n, mv[:, :, 0], mv[:, :, 0], ALU.mult))
            need(pool, e)
            e = sig("norm").on(pool.tensor_tensor(n, n, mv[:, :, 1], ALU.add))
            need(pool, e)
            e = sig("norm").on(pool.tensor_scalar(n, n, float(D), NORM_MIN ** 2, ALU.mult, ALU.max))
            need(pool, e)
            e = sig("norm").on(pool.tensor_tensor(n, n, minus_half[:, :], ALU.pow))
            need(pool, e)
            res["norm"] = sig("norm").on(pool.tensor_scalar(n, n, float(D) ** 0.5, None, ALU.mult))
            yield
            need(act, rstd, y)
            z = {}
            for q in range(TG):
                z[q // 2] = normalise(zs[q], ys[q], q)
                if q % 2:
                    yield
            for pr in range(2):
                xl = transposed(g, pr, "light", zs[2 * pr:2 * pr + 2], z[pr])
                if pr:
                    res["xl"] = xl
                yield

        def router_prep(g, res):
            ys = [y_of[g][:, j, :] for j in range(TG)]
            for j in range(TG):
                t = g * TG + j
                for r in range(2):
                    res["scores"] = sig("score").on(dve.tensor_tensor_reduce(
                        yr[r][:, t, :], ys[j], rt_s[:, r, :], 1.0, 0.0, ALU.mult, ALU.add, scol[:, r, t:t + 1]))
                yield
            for j in range(TG):
                need(act, res["norm"], res["scores"])
                hi = sig("yr_hi").on(act.activation(yr[0][:, g * TG + j, :], ys[j], ACT.Copy, scale=rn[:, g, j:j + 1]))
                if j % 2:
                    yield
            need(dve, hi, res["norm"])
            for j in range(TG):
                t = g * TG + j
                e = sig("yr_lo").on(dve.scalar_tensor_tensor(
                    out=yr[1][:, t, :], in0=ys[j], scalar=rn[:, g, j:j + 1], in1=yr[0][:, t, :].bitcast(F32),
                    op0=ALU.mult, op1=ALU.subtract))
                if j == TG - 1:
                    res["yr"] = e
                if j % 2:
                    yield
            if g == 0:
                last["y_t"] = res["yr"]

        def mixed(a, b, at_):
            for n, _ in enumerate(a):
                yield
                if n >= at_ and next(b, "end") != "end":
                    yield
            yield from b

        def project_light(g, res, banks):
            cols = HALO + g * NG
            jobs = [("q", ch) for ch in range(HC)] + [("k", ch) for ch in range(HC)]
            jobs += [("v", t) for t in (range(0, TG) if g == 0 else range(TG, T + 1))]
            for n, (kind, ch) in enumerate(jobs):
                b = banks[n % len(banks)]
                need(pe, res["xl"], free[b])
                for c in range(C):
                    if kind == "v":
                        w0 = ch * P
                        ins = mm3(bank[b][:, :], [w[:, c, w0:w0 + P] for w in xt],
                                  [w[:, c, 2 * INNER:3 * INNER] for w in wqkv_s], start=(c == 0), stop=(c == C - 1))
                    else:
                        w0 = ch * P + (INNER if kind == "k" else 0)
                        ins = mm3(bank[b][:, :], [w[:, c, w0:w0 + P] for w in wqkv_s],
                                  [w[:, c, cols:cols + NG] for w in xt], start=(c == 0), stop=(c == C - 1))
                e = sig("proj").on(ins)
                last[("xt", 0)] = last[("xt", 1)] = e
                if kind == "q":
                    need(act, e, last.get("gated"))
                    f = sig("q").on(act.activation(qT[:, ch, g * NG:(g + 1) * NG], bank[b][:, :], ACT.Copy, scale=DH ** -0.5))
                elif kind == "k":
                    need(act, e)
                    f = sig("q").on(act.activation(kT[:, ch, cols:cols + NG], bank[b][:, :], ACT.Copy))
                else:
                    need(act, e, *([res["yr"]] if g else []))
                    f = sig("q").on(act.activation(V[:, ch, :], bank[b][:, :], ACT.Copy))
                free[b] = f
                res["qkv"] = f
                yield
            res["proj_done"] = e

        def routing(res):
            for r in range(2):
                for h in range(2):
                    need(pe, res["scores"], free[MISC])
                    for j in range(4):
                        ins = pe.transpose(bank[MISC][:, j * P:(j + 1) * P],
                                           scol[:, r, 4 * h + j:4 * h + j + 1].broadcast_to([P, P]), ident[:, :])
                    e = sig("srow_p").on(ins)
                    need(act, e, res["a1"])
                    row = free[MISC] = sig("srow").on(act.activation(srow[:, r, h * 512:(h + 1) * 512], bank[MISC][:, :], ACT.Copy))
                    yield
            need(dve, row)
            need(dve, last["y_t"])
            last_z = sig("rank_z").on(dve.memset(rank4[:, :, :, :], 0.0))
            need(dve, last_z)
            done = [last_z, last_z]
            for r in range(2):
                for t in range(T):
                    jk, sj = junk[:, t % 2, :], sjunk[:, t % 2, :]
                    need(dve, done[t % 2])
                    s = scol[:, r, t:t + 1]
                    k4 = rank4[:, r, t, :]
                    d = slice(t * P, (t + 1) * P)
                    if t > 0:
                        sig("rank").on(dve.tensor_scalar(jk[:, 0:t * P], srow[:, r, 0:t * P], s, 0.0, ALU.is_gt, ALU.add, accum_out=k4[:, 0:1]))
                    if t < T - 1:
                        sig("rank").on(dve.tensor_scalar(jk[:, (t + 1) * P:N], srow[:, r, (t + 1) * P:N], s, 0.0, ALU.is_ge, ALU.add, accum_out=k4[:, 1:2]))
                    yield
                    sig("rank").on(dve.scalar_tensor_tensor(out=sj[:, 0:P], in0=srow[:, r, d], scalar=s, in1=later[:, :],
                                                            op0=ALU.is_ge, op1=ALU.mult, accum_out=k4[:, 2:3]))
                    e = sig("rank").on(dve.scalar_tensor_tensor(out=sj[:, P:2 * P], in0=srow[:, r, d], scalar=s, in1=not_later[:, :],
                                                                op0=ALU.is_gt, op1=ALU.mult, accum_out=k4[:, 3:4]))
                    done[t % 2] = e
                    yield
                need(dve, e, done[0])
                e = sig("rank").on(dve.tensor_reduce(rank[:, r, :], rank4[:, r, :, :], AX_X, ALU.add))
                if r == 0:
                    rank_q = e
                yield
            ranked = e
            while "proj_done" not in res:
                yield
            for r in range(2):
                need(dve, ranked, done[0], done[1], res["proj_done"])
                for t in range(T):
                    res[f"onehot{r}"] = sig("onehot").on(dve.tensor_scalar(onehots[r][t], iota_row[:, :], rank[:, r, t:t + 1], None, ALU.is_equal))
                    if t % 2:
                        yield
            e = ranked
            res["routed"] = e
            yield
            for h in range(2):
                need(pe, rank_q, free[MISC])
                for j in range(4):
                    ins = pe.transpose(bank[MISC][:, j * P:(j + 1) * P],
                                       rank[:, 0, 4 * h + j:4 * h + j + 1].broadcast_to([P, P]), ident[:, :])
                f = sig("srow_p").on(ins)
                need(act, f, res["routed"])
                free[MISC] = res["rank_row"] = sig("srow").on(act.activation(rank_row[:, h * 512:(h + 1) * 512], bank[MISC][:, :], ACT.Copy))
                yield

        def gather(res, rt):
            for r in range(2):
                b = TP + r
                need(pe, res[f"onehot{r}"], free[b], res["yr"])
                for c in range(C):
                    for t in range(T):
                        for part in range(2):
                            ins = pe.matmul(bank[b][:, c * NSEL:(c + 1) * NSEL], yr[part][:, t, c * P:(c + 1) * P], onehots[r][t],
                                            start=(t == 0 and part == 0), stop=(t == T - 1 and part == 1))
                oh_used = sig("gather").on(ins)
                need(act, oh_used, res["proj_done"])
                for c in range(C):
                    f = sig("hin").on(act.activation(hin[r][:, c, :], bank[b][:, c * NSEL:(c + 1) * NSEL], ACT.Copy, scale=gam_s[:, c:c + 1]))
                free[b] = f
                res[f"hin{r}"] = f
            res["x_free"] = oh_used
            n = 0
            for kind in ("q", "k"):
                w, r, dst = (wqh_s, 0, hq) if kind == "q" else (wkvh_s, 1, hk)
                for pr in range(2):
                    b = n % 4
                    need(pe, res[f"hin{r}"], free[b])
                    for j in range(2):
                        ch = 2 * pr + j
                        for c in range(C):
                            ins = pe.matmul(bank[b][:, j * NSEL:(j + 1) * NSEL], w[:, c, ch * P:(ch + 1) * P], hin[r][:, c, :],
                                            start=(c == 0), stop=(c == C - 1))
                    e = sig("hproj").on(ins)
                    need(act, e, res["proj_done"])
                    free[b] = res["hqkv"] = sig("hqkv").on(act.activation(
                        dst[:, 2 * pr:2 * pr + 2, :], bview(b, "p (j n) -> p j n", j=2), ACT.Copy,
                        scale=DH ** -0.5 if kind == "q" else 1.0))
                    n += 1
            for t in range(ST):
                b = n % 4
                need(pe, res["hin1"], free[b])
                for c in range(C):
                    ins = pe.matmul(bank[b][:, :], hin[1][:, c, t * P:(t + 1) * P], wkvh_s[:, c, INNER:2 * INNER],
                                    start=(c == 0), stop=(c == C - 1))
                e = sig("hproj").on(ins)
                need(act, e)
                free[b] = res["hqkv"] = sig("hqkv").on(act.activation(hv[:, t, :], bank[b][:, :], ACT.Copy))
                n += 1
            finish(rt)
            need(dve, res["rank_row"], oh_used)
            for kk in range(ST):
                res["rank_hot"] = sig("rank_hot").on(dve.tensor_scalar(rank_hot[:, kk, :], rank_row[:, :], iota_col[:, kk:kk + 1], None, ALU.is_equal))

        def attention(tiles, between, tile_done):
            items = [(n, hp) for n in range(len(tiles)) for hp in range(HEADS // 2)]
            soft, turned = {}, {}
            prob_free, probT_free = {}, {}
            o_ready, normed_of = {}, {}

            def head(hp, h):
                return hp // 2 * 4 + hp % 2 + 2 * h

            def scores(i):
                n, hp = items[i]
                tl = tiles[n]
                b = i % 2
                if hp == 0 and "before" in tl:
                    tl["before"]()
                need(pe, tl["ready"](), free[b])
                sv = bview(b, "p (h k) -> p h k", h=2)
                for h in range(2):
                    hs, ch = slice(hp % 2 * DH, (hp % 2 + 1) * DH), head(hp, h) // 2
                    ins = pe.matmul(sv[:, h, :], tl["q"](hs, ch), tl["k"](hs, ch),
                                    start=True, stop=True)
                e = sig("sim").on(ins)
                need(dve, e, soft.get(i - 4))
                pr = prob[i % NP]
                if tl["mask"] is None:
                    m = sig("nmax").on(dve.tensor_reduce(nmax[:, i % 4, :], sv, AX_X, ALU.max, negate=True))
                    src, sign = sv, 1.0
                else:
                    need(dve, prob_free.get(i - NP), last["ring"])
                    for h in range(2):
                        m = sig("nmax").on(dve.tensor_tensor_reduce(pr[:, h, :], sv[:, h, :], mask[:, tl["mask"], :], -1.0, 3e38,
                                                                    ALU.add, ALU.min, nmax[:, i % 4, h:h + 1]))
                    src, sign = pr, -1.0
                    free[b] = m
                need(act, m, prob_free.get(i - NP), last["ring"])
                if hp == 0:
                    need(act, normed_of.get(n - 2))
                for h in range(2):
                    e = sig("soft").on(act.activation(pr[:, h, :], src[:, h, :], ACT.Exp, bias=nmax[:, i % 4, h:h + 1], scale=sign,
                                                      accum_out=den[:, n % 2, head(hp, h):head(hp, h) + 1]))
                soft[i] = e
                if tl["mask"] is None:
                    free[b] = e

            def turn(i):
                b = 2 + i % 2
                need(pe, soft[i], free[b])
                for h in range(2):
                    for kk in range(2):
                        ins = pe.transpose(bank[b][:, (2 * h + kk) * P:(2 * h + kk + 1) * P],
                                           prob[i % NP][:, h, kk * P:(kk + 1) * P], ident[:, :])
                e = prob_free[i] = sig("probT_p").on(ins)
                src = bview(b, "p (a n) -> p a n", a=4)
                need(act, e, probT_free.get(i - 2), last["ring"])
                free[b] = turned[i] = sig("probT_a").on(act.activation(probT[i % 2][:, :, :], src, ACT.Copy))

            def values(i):
                n, hp = items[i]
                b = 4 + n % 2
                need(pe, turned[i])
                if hp == 0:
                    need(pe, free[b])
                for h in range(2):
                    hd = head(hp, h)
                    for kk in range(2):
                        ins = pe.matmul(bank[b][:, hd * DH:(hd + 1) * DH], probT[i % 2][:, 2 * h + kk, :], tiles[n]["v"](kk, hd),
                                        start=(kk == 0), stop=(kk == 1))
                e = probT_free[i] = sig("pv").on(ins)
                if hp == HEADS // 2 - 1:
                    need(dve, soft[i], last.get("rden"))
                    r = sig("rden").on(dve.reciprocal(rden[:, :], den[:, n % 2, :]))
                    need(dve, e, r, last.get("o_s"), last["ring"])
                    f = sig("o").on(dve.tensor_tensor(o_s[:, :].rearrange("p (h d) -> p h d", h=HEADS),
                                                      bview(b, "p (h d) -> p h d", h=HEADS),
                                                      rden[:, :].unsqueeze(2).broadcast_to([P, HEADS, DH]), ALU.mult))
                    last["rden"] = free[b] = o_ready[n] = normed_of[n] = f

            def out_turn(n):
                need(pe, o_ready[n], free[TP])
                for ch in range(HC):
                    ins = pe.transpose(bank[TP][:, ch * P:(ch + 1) * P], o_s[:, ch * P:(ch + 1) * P], ident[:, :])
                e = last["o_s"] = sig("oT_p").on(ins)
                need(act, e, last.get("oT_s"), last["ring"])
                f = free[TP] = sig("oT").on(act.activation(oT_s[:, :, :], bview(TP, "p (c n) -> p c n", c=HC), ACT.Copy))
                return f

            def out_proj(n, f):
                tl = tiles[n]
                if n == 0:
                    pe.wait_ge(late_loaded, late)
                need(pe, f, free[TP], *tl["extra_ready"]())
                ins = None
                for ch in range(HC):
                    ins = pe.matmul(bank[TP][:, 0:D], oT_s[:, ch, :], tl["wo"][:, ch, :], start=(ch == 0),
                                    stop=(ch == HC - 1 and not tl["extra"]))
                more = tl["extra"]
                for m, (lh, rh) in enumerate(more):
                    ins = pe.matmul(bank[TP][:, 0:D], lh, rh, start=False, stop=(m == len(more) - 1))
                e = last["oT_s"] = sig("y_out").on(ins)
                free[TP] = tl["sink"](bank[TP][:, 0:D], e)
                tile_done(n, free[TP])

            pend = []
            L = len(items)
            for s in range(L + 7):
                between(s)
                if 0 <= s - 2 < L:
                    turn(s - 2)
                if s < L:
                    scores(s)
                if 0 <= s - 3 < L:
                    values(s - 3)
                    if items[s - 3][1] == HEADS // 2 - 1:
                        pend.append((s, items[s - 3][0]))
                if pend and pend[0][0] + 1 == s:
                    oT_ev = out_turn(pend[0][1])
                if pend and pend[0][0] + 2 == s:
                    out_proj(pend.pop(0)[1], oT_ev)
            assert not pend
            return (sig("pv").sem, sig("pv").n)

        def row(b, peeled):
            res = [dict(first), {}]
            fill = chain(gates_turned(0, res[0]), ffn_prep(1, xin, [], res[1]), route_and_turn(1, res[1]))
            a0 = ffn_main(0, xin, x1, res[0], fill, "ffn1_0", stored_before=b * 16 + 16)
            xl0, ares = {}, {}
            until(fill, res[1], "xt")
            score0 = router_prep(0, xl0)
            fill = chain(fill, light_prep(0, [a0], xl0))
            a1 = ffn_main(1, xin, x1, res[1], chain(fill, score0), "ffn1_1", stored_before=b * 16 + 16)
            until(fill, xl0, "xl")
            ares["x_free"] = ares["a1"] = a1
            last["ring"] = last[("h", (E - 1) % NH)]
            rt = chain(mixed(light_prep(1, [a1], ares), score0, 0), router_prep(1, ares), routing(ares))
            advance(rt, PACE["attn"][0])
            for n, _ in enumerate(project_light(0, xl0, (0, 1, 2, 3))):
                advance(rt, PACE["project_0"][n])
            until(rt, ares, "yr")
            project = project_light(1, ares, (MISC,))
            advance(project, PACE["project_1"][-1])
            res2 = [{}, {}]
            summed, preps = {}, {}

            def scatter(t):
                return [(rank_hot[:, kk, t * P:(t + 1) * P], ho[part][:, kk, :]) for kk in range(ST) for part in range(2)]

            def light(t, fused):
                def sink(y, e):
                    need(dve, e)
                    summed[t] = sig("x2").on(dve.tensor_tensor(x1[:, t, :], y, x1[:, t, :], ALU.add))
                    return summed[t]
                return dict(
                    name=t, ready=lambda: (xl0 if t < TG - 1 else ares)["qkv"], mask=0 if t == 0 else 2 if t == T - 1 else 1, wo=wol_s, sink=sink,
                    extra=scatter(t) if fused else [],
                    extra_ready=lambda: [ares["ho"], ares["rank_hot"]] if fused else [],
                    q=lambda hs, ch: qT[hs, ch, t * P:(t + 1) * P],
                    k=lambda hs, ch: kT[hs, ch, t * P:t * P + KEYS],
                    v=lambda kk, hd: V[:, t + kk, hd * DH:(hd + 1) * DH])

            def start_heavy():
                until(rt, ares, "routed")
                pe.wait_ge(late_loaded, late)
                gather(ares, rt)
                if not peeled:
                    need(sp, ares["x_free"])
                    for g in range(G):
                        x_next[g] = sig(f"x_load{g}").on(sp.dma_start(xin[:, g * TG:(g + 1) * TG, :], x_next_src(b, g)), 16)

            def heavy(n):
                def sink(y, e):
                    need(act, e, ares["rank_hot"])
                    hi = sig("ho_hi").on(act.activation(ho[0][:, n, :], y, ACT.Copy))
                    need(dve, hi)
                    ares["ho"] = sig("ho_lo").on(dve.tensor_tensor(ho[1][:, n, :], y, ho[0][:, n, :].bitcast(F32), ALU.subtract))
                    return ares["ho"]
                tl = dict(
                    name=f"heavy{n}", ready=lambda: ares["hqkv"], mask=None, wo=woh_s, extra=[], extra_ready=lambda: [], sink=sink,
                    q=lambda hs, ch: hq[hs, ch, n * P:(n + 1) * P],
                    k=lambda hs, ch: hk[hs, ch, :],
                    v=lambda kk, hd: hv[:, kk, hd * DH:(hd + 1) * DH])
                if n == 0:
                    tl["before"] = start_heavy
                return tl

            EARLY = T - 4
            tiles = [light(t, False) for t in range(EARLY)] + [heavy(n) for n in range(ST)]
            tiles += [light(t, True) for t in range(EARLY, T)]

            def between(s):
                if s < (TG - 1) * HEADS // 2:
                    advance(project, PACE["project_1"][s])
                elif s == (TG - 1) * HEADS // 2:
                    finish(project)
                if s < EARLY * HEADS // 2:
                    advance(rt, PACE["routing"][s])
                elif 0 in preps:
                    advance(preps[0], PACE["ffn2_prep"][s - (T + ST - 4) * HEADS // 2])

            def tile_done(n, e):
                name = tiles[n]["name"]
                if name == f"heavy{ST - 1}":
                    last[("xt", 0)] = last[("xt", 1)] = e
                    for pr in range(EARLY // 2):
                        sbk = (MISC, TP)[pr % 2]
                        need(pe, ares["ho"], ares["rank_hot"], free[sbk])
                        for j in range(2):
                            parts = scatter(2 * pr + j)
                            for m, (lh, rh) in enumerate(parts):
                                ins = pe.matmul(bank[sbk][:, j * D:(j + 1) * D], lh, rh, start=(m == 0), stop=(m == len(parts) - 1))
                        e = sig("scatter").on(ins)
                        need(dve, e, summed[2 * pr + 1])
                        e = free[sbk] = sig("x2").on(dve.tensor_tensor(x1[:, 2 * pr:2 * pr + 2, :], bview(sbk, "p (t n) -> p t n", t=2),
                                                                        x1[:, 2 * pr:2 * pr + 2, :], ALU.add))
                    preps[0] = chain(ffn_prep(0, x1, [e], res2[0]), route_and_turn(0, res2[0]))
                if name == T - 1:
                    until(preps[0], res2[0], "xt")
                    preps[1] = chain(ffn_prep(1, x1, [e], res2[1]), route_and_turn(1, res2[1]))

            in_use["TP"] = True
            att = attention(tiles, between, tile_done)
            in_use["TP"] = False
            need(act, att)
            need(pool, att)
            f0 = ffn_main(0, x1, x1, res2[0], chain(preps[0], preps[1]), "ffn2_0")
            need(sp, f0)
            store(b, 0)
            nxt = {}
            until(preps[1], res2[1], "xt")
            prep = iter(()) if peeled else ffn_prep(0, xin, [x_next[0]], nxt)
            if not peeled:
                prep = chain(prep, ffn_route(0, nxt))
            fill = chain(preps[1], prep)
            f1 = ffn_main(1, x1, x1, res2[1], fill, "ffn2_1")
            if not peeled:
                finish(fill)
            need(sp, f1)
            store(b, 1)
            if not peeled:
                need(dve, x_next[1])

        x_next = {}

        def x_next_src(b, g):
            return x_v[bass.ds(b + 1, 1), :, g * TG:(g + 1) * TG, :].rearrange("b p t d -> p (b t) d")

        def store(b, g):
            gs = slice(g * TG, (g + 1) * TG)
            if isinstance(b, int):
                dst = out_v[b, :, gs, :]
            else:
                dst = out_v[bass.ds(b, 1), :, gs, :].rearrange("b p t d -> p (b t) d")
            sp.dma_start(dst, x1[:, gs, :]).then_inc(stored[g], 16)

        def new_counts():
            nc.all_engine_barrier()
            pool.sem_clear(clear_range())
            nc.all_engine_barrier()
            for s in sems.values():
                s.n = 0
            waited.clear()
            last.clear()
            for i in range(8):
                free[i] = None

        def clear_range():
            nums = sorted(s.sem.num for s in sems.values())
            assert nums == list(range(nums[0], nums[-1] + 1)), nums
            return range(nums[0], nums[-1] + 1)

        for e_ in (pe, act, dve, pool):
            need(e_, consts)
        first = {}
        prep, splits = ffn_prep(0, xin, [x_ready[0]], first), split_weights()
        prep = chain(prep, ffn_route(0, first))
        need(dve, bias_loaded)
        for n_prep, n_split in PACE["start"]:
            advance(prep, n_prep)
            advance(splits, n_split)
        finish(prep)
        finish(splits)
        need(pool, res_w["split"])
        for side in (slice(0, HALO), slice(HALO + N, PADDED)):
            k.on(pool.memset(kT[:, :, side], 0.0))
        need(act, bias_loaded)
        need(dve, x_ready[1])
        names = ("gated acc_p gT_hi xl_f xl_lo norm norm_a score yr_hi yr_lo hidden gelu h_lo expert acc bias2 proj q srow_p srow rank_z rank "
                 "onehot gather hin rank_hot hproj hqkv sim nmax soft probT_p probT_a pv rden o oT_p oT y_out ho_hi ho_lo x2 scatter").split()
        for n_ in names:
            sig(n_)
        new_counts()
        first = dict.fromkeys(("xt", "gate"))
        with nc.Fori(0, ROWS - 1) as b:
            row(b, False)
            new_counts()
        row(ROWS - 1, True)
        for s_ in stored:
            sp.wait_ge(s_, 16 * ROWS + 16)
        nc.all_engine_barrier()


_INS = ["L0_attn_x", "L0_attn_gamma_h", "L0_attn_wq_h", "L0_attn_wkv_h", "L0_attn_wo_h", "L0_attn_ln_g", "L0_attn_ln_b",
        "L0_attn_wqkv_l", "L0_attn_wo_l", "L0_attn_rt_q", "L0_attn_rt_kv", "L0_ffn_router_w", "L0_ffn_router_b",
        "L0_ffn_W1", "L0_ffn_b1", "L0_ffn_W2", "L0_ffn_b2"]


def kernel(**inputs):
    import concourse.bacc as bacc
    from concourse.bass_utils import run_bass_kernel_spmd

    nc = bacc.Bacc("TRN2", target_bir_lowering=False, num_devices=1)
    arrays, args = {}, []
    for name in _INS:
        a = np.ascontiguousarray(inputs[name])
        arrays[f"in_{name}"] = a
        args.append(nc.dram_tensor(f"in_{name}", a.shape, mybir.dt.from_np(a.dtype), kind="ExternalInput").ap())
    shape = arrays["in_L0_attn_x"].shape
    args.append(nc.dram_tensor("out_0", shape, F32, kind="ExternalOutput").ap())
    build(nc, *args)
    r = run_bass_kernel_spmd(nc, [arrays], core_ids=[0])
    return r.results[0]["out_0"]
```
